# Optimizing a Trainium2 kernel written in Bass

```python
import numpy as np
import jax
import jax.numpy as jnp

def _softmax(x, axis=-1):
    return jax.nn.softmax(x, axis=axis)
def _gelu(x):
    return jax.nn.gelu(x, approximate=True)
def _silu(x):
    return jax.nn.silu(x)
def _sigmoid(x):
    return jax.nn.sigmoid(x)
def _layernorm(x, axis=-1, eps=1e-5):
    m = jnp.mean(x, axis=axis, keepdims=True)
    v = jnp.var(x, axis=axis, keepdims=True)
    return (x - m) / jnp.sqrt(v + eps)
def _scatter_add(tgt, idx, src, axis=0):
    return tgt.at[idx].add(src)
def _segment_sum(src, seg, n):
    return jax.ops.segment_sum(src, seg, n)

kernel_name = 'mk_adj_resnorm_d2_adj_256_7986ce'

def setup_inputs(seed: int = 0):
    np.random.seed(seed)
    _w = jnp.asarray
    def _rec_inputs():
        import jax
        import jax.numpy as jnp
        _gk = jax.random.key(seed)
        x = -0.000929 + 1 * jax.random.normal(jax.random.fold_in(_gk, 1), (4096, 256), jnp.float32)
        _a = jax.random.bernoulli(jax.random.fold_in(_gk, 2), 0.00390625, (4096, 4096))
        _a = jnp.logical_or(_a, jnp.swapaxes(_a, -1, -2))
        _a = jnp.logical_or(_a, jnp.eye(4096, dtype=bool))
        adj = _a.astype(jnp.int32)
        return x, adj
    x, adj = _rec_inputs()
    def _L0_gnn_setup():
        import jax, jax.numpy as jnp
        import numpy as np
        N, F_IN, NHID, NHEADS, OUTDIM = (4096, 256, 128, 8, 256)
        ALPHA = 0.2
        NEG = -9000000000000000.0

        def _gat(x, adj, W_heads, a1, a2, W_out, b_out):
            Wh = jnp.einsum('nf,hfd->hnd', x, W_heads)
            s1 = jnp.einsum('hnd,hd->hn', Wh, a1)
            s2 = jnp.einsum('hnd,hd->hn', Wh, a2)
            e = s1[:, :, None] + s2[:, None, :]
            e = jnp.where(e > 0, e, ALPHA * e)
            e = jnp.where(adj[None, :, :] > 0, e, NEG)
            att = jax.nn.softmax(e, axis=-1)
            hp = jnp.einsum('hnm,hmd->hnd', att, Wh)
            hp = jax.nn.elu(hp)
            feat = jnp.transpose(hp, (1, 0, 2)).reshape(N, NHEADS * NHID)
            return feat @ W_out + b_out
        key = jax.random.key(seed)
        ks = jax.random.split(key, 7)
        x = jax.random.normal(ks[0], (N, F_IN), jnp.float32)
        adj = jax.random.randint(ks[1], (N, N), 0, 2, jnp.int32)
        W_heads = jax.random.normal(ks[2], (NHEADS, F_IN, NHID), jnp.float32) * (1.414 / np.sqrt(F_IN))
        a1 = jax.random.normal(ks[3], (NHEADS, NHID), jnp.float32) * 0.1
        a2 = jax.random.normal(ks[4], (NHEADS, NHID), jnp.float32) * 0.1
        W_out = jax.random.normal(ks[5], (NHID * NHEADS, OUTDIM), jnp.float32) * (1.0 / np.sqrt(NHID * NHEADS))
        b_out = jnp.zeros((OUTDIM,), jnp.float32)
        return {'x': x, 'adj': adj, 'W_heads': W_heads, 'a1': a1, 'a2': a2, 'W_out': W_out, 'b_out': b_out}
    _L0_gnn_all = _L0_gnn_setup()
    _L0_gnn_in = {k: v for k, v in _L0_gnn_all.items() if k in ('W_heads', 'a1', 'a2', 'W_out', 'b_out', )}
    del _L0_gnn_all

    def _L1_gnn_setup():
        import jax, jax.numpy as jnp
        import numpy as np
        N = 4096
        IN_F = 256
        OUT_F = 64
        HEADS = 4
        NEG_SLOPE = 0.2
        key = jax.random.key(seed)
        k1, k2, k3, k4 = jax.random.split(key, 4)
        x = jax.random.normal(k1, (N, IN_F), dtype=jnp.float32)
        W = jax.random.normal(k2, (HEADS, IN_F, OUT_F), dtype=jnp.float32) * (1.0 / np.sqrt(IN_F))
        a = jax.random.normal(k3, (HEADS, 2 * OUT_F), dtype=jnp.float32) * (1.0 / np.sqrt(2 * OUT_F))
        adj_matrix = jax.random.randint(k4, (N, N), 0, 2, dtype=jnp.int32)
        return {'x': x, 'W': W, 'a': a, 'adj_matrix': adj_matrix}
    _L1_gnn_all = _L1_gnn_setup()
    _L1_gnn_in = {k: v for k, v in _L1_gnn_all.items() if k in ('W', 'a', )}
    del _L1_gnn_all

    return {
        "x": x,
        "adj": adj,
        "L0_gnn_W_heads": _L0_gnn_in["W_heads"],
        "L0_gnn_a1": _L0_gnn_in["a1"],
        "L0_gnn_a2": _L0_gnn_in["a2"],
        "L0_gnn_W_out": _L0_gnn_in["W_out"],
        "L0_gnn_b_out": _L0_gnn_in["b_out"],
        "L1_gnn_W": _L1_gnn_in["W"],
        "L1_gnn_a": _L1_gnn_in["a"],
    }

def reference(x, adj, L0_gnn_W_heads, L0_gnn_a1, L0_gnn_a2, L0_gnn_W_out, L0_gnn_b_out, L1_gnn_W, L1_gnn_a):
    import jax
    import jax.numpy as jnp
    def _L0_gnn_ref(x, adj, W_heads, a1, a2, W_out, b_out):
        import jax, jax.numpy as jnp
        import numpy as np
        N, F_IN, NHID, NHEADS, OUTDIM = (4096, 256, 128, 8, 256)
        ALPHA = 0.2
        NEG = -9000000000000000.0

        def _gat(x, adj, W_heads, a1, a2, W_out, b_out):
            Wh = jnp.einsum('nf,hfd->hnd', x, W_heads)
            s1 = jnp.einsum('hnd,hd->hn', Wh, a1)
            s2 = jnp.einsum('hnd,hd->hn', Wh, a2)
            e = s1[:, :, None] + s2[:, None, :]
            e = jnp.where(e > 0, e, ALPHA * e)
            e = jnp.where(adj[None, :, :] > 0, e, NEG)
            att = jax.nn.softmax(e, axis=-1)
            hp = jnp.einsum('hnm,hmd->hnd', att, Wh)
            hp = jax.nn.elu(hp)
            feat = jnp.transpose(hp, (1, 0, 2)).reshape(N, NHEADS * NHID)
            return feat @ W_out + b_out
        return _gat(x, adj, W_heads, a1, a2, W_out, b_out)

    def _L1_gnn_ref(x, W, a, adj_matrix):
        import jax, jax.numpy as jnp
        import numpy as np
        N = 4096
        IN_F = 256
        OUT_F = 64
        HEADS = 4
        NEG_SLOPE = 0.2
        heads, in_f, out_f = W.shape
        n = x.shape[0]
        xt = jnp.einsum('ni,hio->hno', x, W)
        src = jnp.einsum('hnf,hf->hn', xt, a[:, :out_f])
        dst = jnp.einsum('hnf,hf->hn', xt, a[:, out_f:])
        e = jax.nn.leaky_relu(src[:, :, None] + dst[:, None, :], NEG_SLOPE)
        mask = (adj_matrix > 0)[None, :, :]
        e = jnp.where(mask, e, -jnp.inf)
        attention = jax.nn.softmax(e, axis=2)
        h_prime = jnp.einsum('hij,hjf->hif', attention, xt)
        return h_prime.transpose(1, 0, 2).reshape(n, heads * out_f)

    x = _layernorm(x + _L0_gnn_ref(x, adj, L0_gnn_W_heads, L0_gnn_a1, L0_gnn_a2, L0_gnn_W_out, L0_gnn_b_out), axis=-1)
    x = _layernorm(x + _L1_gnn_ref(x, L1_gnn_W, L1_gnn_a, adj), axis=-1)
    return x


_drawn_inputs = setup_inputs


def setup_inputs(seed=0):
    import zlib

    import numpy as np

    out = dict(_drawn_inputs(seed))
    spreads = {'L0_gnn_b_out': (0.0, 0.1)}
    factors = {}
    for name, (base, spread) in spreads.items():
        noise = np.random.default_rng([zlib.crc32(name.encode()), seed]).standard_normal(out[name].shape)
        drawn = base * np.exp(spread * noise) if base else spread * noise
        out[name] = jnp.asarray(drawn.astype(out[name].dtype))
    for name, factor in factors.items():
        out[name] = (out[name] * factor).astype(out[name].dtype)
    return out
```

```python
from contextlib import ExitStack

import numpy as np

import concourse.bass as bass
from concourse import mybir

P = 128
F32 = mybir.dt.float32
F16 = mybir.dt.float16
F8 = mybir.dt.float8e4
I32 = mybir.dt.int32
U32 = mybir.dt.uint32
U8 = mybir.dt.uint8
ALU = mybir.AluOpType
ACT = mybir.ActivationFunctionType
AX = mybir.AxisListType
ABSMAX = bass.bass_isa.ReduceOp.absmax
RMAX = bass.bass_isa.ReduceOp.max

BANK = 512
BLK = 512
TPB = BLK // P
CPB = 8
NBUF = 4
SLOPE = 0.2
STEEP = 2.0 ** 64
ONE8 = 0x38
ONE8X4 = 0x38383838
LN_EPS = 1e-5
SWEEP = [list(range(CPB)), list(range(CPB))[::-1]]
MAKE = [0, 1, 7, 6, 2, 3, 4, 5]
PE_OFFSET = 1024


class Scope:

    def __init__(self, nc, ctx, tag):
        self.nc, self.ctx, self.tag = nc, ctx, tag

    def sb(self, name, shape, dt):
        return self.ctx.enter_context(self.nc.sbuf_tensor(f"{self.tag}_{name}", shape, dt))

    def ps(self, name, shape):
        return self.ctx.enter_context(self.nc.psum_tensor(f"{self.tag}_{name}", shape, F32))

    def sem(self, name):
        return self.ctx.enter_context(self.nc.semaphore(f"{self.tag}_{name}"))


class Chain:

    def __init__(self, eng, sem, base=0):
        self.eng, self.sem, self.base, self.n = eng, sem, base, 0

    def mark(self, ins):
        ins.then_inc(self.sem, 1)
        self.n += 1
        return self.base + self.n

    def wait(self, value):
        self.eng.wait_ge(self.sem, value)

    def link(self, ins):
        self.wait(self.mark(ins))


def held(eng, pad):
    eng.sem_inc(pad, 1)


def make_identity(nc, pool, tile, sem):
    nc.gpsimd.memset(tile[:, :], 1.0).then_inc(sem, 1)
    pool.wait_ge(sem, 1)
    nc.gpsimd.affine_select(out=tile[:, :], in_=tile[:, :], compare_op=ALU.is_equal, fill=0.0, base=0,
                            pattern=[[-1, P]], channel_multiplier=1).then_inc(sem, 1)


def mask_phase(nc, adj, mask_t):
    N = adj.shape[0]
    NT = N // P
    per_bank = BANK // P
    banks = NT // per_bank
    nps = min(8, banks)
    act_banks = [k for k in range(banks) if k % 2 == 0]
    dve_banks = [k for k in range(banks) if k % 2 == 1]
    na, nd = len(act_banks), len(dve_banks)
    with ExitStack() as ctx:
        s = Scope(nc, ctx, "mk")
        rows = [s.sb(f"rows{p}", [P, N], I32) for p in range(2)]
        ident = s.sb("ident", [P, P], F32)
        stage = [s.sb(f"stage{k}", [P, BANK], F8) for k in range(na)]
        banks_ps = [s.ps(f"b{k}", [P, BANK]) for k in range(nps)]
        s_id, s_tr = s.sem("id"), s.sem("tr")
        s_ld = [s.sem(f"ld{p}") for p in range(2)]
        s_act, s_dve, s_stg, s_pad = s.sem("act"), s.sem("dve"), s.sem("stg"), s.sem("pad")
        block = ctx.enter_context(nc.Block())

        @block.gpsimd
        def _(pool):
            make_identity(nc, pool, ident, s_id)

        @block.sync
        def _(sp):
            def load(it, p):
                sp.dma_start(rows[p][:, :], adj[bass.ds(it * P, P), :]).then_inc(s_ld[p], 16)
            for p in range(2):
                load(p, p)
            with sp.Fori(1, NT // 2) as i2:
                for p in range(2):
                    sp.wait_ge(s_tr, (2 * i2 + p - 1) * banks)
                    load(2 * i2 + p, p)

        @block.tensor
        def _(pe):
            pe.wait_ge(s_id, 2)

            def row(i2, p, first):
                it = 2 * i2 + p
                pe.wait_ge(s_ld[p], 16 * (i2 + 1))
                for k in range(banks):
                    if not first:
                        if k in act_banks:
                            pe.wait_ge(s_act, (it - 1) * na + (act_banks.index(k) + 1))
                        else:
                            pe.wait_ge(s_dve, (it - 1) * nd + (dve_banks.index(k) + 1))
                    for r in range(per_bank):
                        jt = k * per_bank + r
                        last = nc.tensor.transpose(banks_ps[k][:, r * P:(r + 1) * P],
                                                   rows[p][:, jt * P:(jt + 1) * P].bitcast(F32), ident[:, :])
                    last.then_inc(s_tr, 1)
            row(0, 0, True)
            row(0, 1, False)
            with pe.Fori(1, NT // 2) as i2:
                for p in range(2):
                    row(i2, p, False)

        @block.scalar
        def _(act):
            with act.Fori(0, NT) as it:
                for m, k in enumerate(act_banks):
                    act.wait_ge(s_stg, it * na + m)
                    act.wait_ge(s_tr, it * banks + k + 1)
                    held(act, s_pad)
                    act.activation(stage[m][:, :], banks_ps[k][:, :].bitcast(I32), ACT.Relu, scale=STEEP,
                                   saturate=False).then_inc(s_act, 1)

        @block.vector
        def _(dve):
            with dve.Fori(0, NT) as it:
                for k in range(banks):
                    cols = lambda t, w: t[:, k * per_bank:(k + 1) * per_bank, bass.ds(it * (P // w), P // w)]
                    if k in dve_banks:
                        dve.wait_ge(s_tr, it * banks + k + 1)
                        dve.tensor_scalar(cols(mask_t, 1),
                                          banks_ps[k][:, :].bitcast(I32).rearrange("p (r i) -> p r i", r=per_bank),
                                          0.0, float(ONE8), ALU.is_gt, ALU.mult).then_inc(s_dve, 1)
                    else:
                        m = act_banks.index(k)
                        dve.wait_ge(s_act, it * na + m + 1)
                        dve.tensor_scalar(cols(mask_t[:, :, :].bitcast(U32), 4),
                                          stage[m][:, :].bitcast(U32).rearrange("p (r i) -> p r i", r=per_bank),
                                          ONE8X4, None, ALU.bitwise_and).then_inc(s_stg, 1)


def prep_phase(nc, tag, x, W, a1, a2, d, facs):
    N, F = x.shape
    H, _, D = W.shape
    HD, NT, KT = H * D, N // P, F // P
    G = 4
    NG = NT // G
    halves = max(1, HD // BANK)
    HW = HD // halves
    with ExitStack() as ctx:
        s = Scope(nc, ctx, tag)
        wall = s.sb("wall", [P, KT, HD + 2 * H], F32)
        abc = s.sb("abc", [P, 2, HD], F32)
        prod = s.sb("prod", [P, HD], F32)
        xin = [s.sb(f"xin{p}", [P, G, F], F32) for p in range(2)]
        xt = s.sb("xt", [P, G, KT, P], F32)
        whs = [s.sb(f"whs{p}", [P, HD], F32) for p in range(2)]
        scg = [s.sb(f"scg{p}", [P, G, 2 * H], F32) for p in range(2)]
        scol = s.sb("scol", [P, NT, 2 * H], F32)
        rows = [s.sb(f"rows{p}", [H, G * P], F32) for p in range(2)]
        ident = s.sb("ident", [P, P], F32)
        ones = s.sb("ones", [P, P], F32)
        xacc = s.sb("xacc", [P, F], F32)
        xpart = s.sb("xpart", [P, F], F32)
        xmean = s.sb("xmean", [P, KT, P], F32)
        means = s.sb("means", [P, HD], F32)
        ext = s.sb("ext", [P, NG], F32)
        big = s.sb("big", [P, 2], F32)
        bigr = s.sb("bigr", [P, 2], F32)
        lam = s.sb("lam", [P, 4], F32)
        smax = s.sb("smax", [P, H], F32)
        smaxr = s.sb("smaxr", [P, H], F32)
        ta = s.sb("ta", [P, H, NT], F32)
        tb = s.sb("tb", [P, H, NT], F32)
        tu = s.sb("tu", [P, H, NT], F32)
        tv = s.sb("tv", [P, H, NT], F32)
        kc = s.sb("kc", [P, H, NT], F32)
        ps_t = s.ps("pst", [P, G, KT, P])
        ps_w = [[s.ps(f"psw{p}{k}", [P, BANK]) for k in range(halves)] for p in range(2)]
        ps_s = s.ps("pss", [P, BANK])
        ps_r = s.ps("psr", [P, BANK])
        s_w = s.sem("w")
        s_id = s.sem("id")
        s_wa = s.sem("wa")
        s_x = [s.sem(f"x{p}") for p in range(2)]
        s_tp = s.sem("tp")
        s_ta, s_td = s.sem("ta"), s.sem("td")
        s_mm = s.sem("mm")
        s_wc, s_wd = s.sem("wc"), s.sem("wd")
        s_sc = s.sem("sc")
        s_rt, s_rc = s.sem("rt"), s.sem("rc")
        s_xr = s.sem("xr")
        s_wo = [s.sem(f"wo{p}") for p in range(2)]
        s_ro = [s.sem(f"ro{p}") for p in range(2)]
        s_ch = s.sem("ch")
        s_f = s.sem("f")
        s_ar = s.sem("ar")
        s_ex = s.sem("ex")
        s_xm, s_xc, s_mn, s_mc = (s.sem(n) for n in ("xm", "xc", "mn", "mc"))
        s_o = s.sem("o")
        block = ctx.enter_context(nc.Block())

        @block.gpsimd
        def _(pool):
            make_identity(nc, pool, ident, s_id)
            nc.gpsimd.memset(ones[:, :], 1.0).then_inc(s_id, 1)
            pool.wait_ge(s_f, 1)
            nc.gpsimd.partition_all_reduce(bigr[:, :], big[:, :], P, ABSMAX).then_inc(s_ar, 1)
            pool.wait_ge(s_f, 2)
            nc.gpsimd.partition_all_reduce(smaxr[:, :], smax[:, :], P, RMAX).then_inc(s_ar, 1)

        @block.sync
        def _(sp):
            for k in range(KT):
                sp.dma_start(wall[:, k, 0:HD].rearrange("p (h e) -> p h e", h=H),
                             W[:, k * P:(k + 1) * P, :].rearrange("h p e -> p h e")).then_inc(s_w, 16)
            for m, a in enumerate((a1, a2)):
                sp.dma_start(abc[:, m, :].rearrange("p (h e) -> p h e", h=H),
                             a.unsqueeze(0).to_broadcast([P, H, D])).then_inc(s_w, 16)
            xg = x.rearrange("(g p) f -> p g f", p=P)

            def load(g, p):
                sp.dma_start(xin[p][:, :, :], xg[:, bass.ds(g * G, G), :]).then_inc(s_x[p], 16)

            def store(g2, p):
                g = 2 * g2 + p
                for u in range(G):
                    t = g * G + u
                    sp.wait_ge(s_wc, t + 3)
                    if halves > 1:
                        sp.wait_ge(s_wd, t + 3)
                    sp.dma_start(d["wh"][bass.ds(t * P, P), :], whs[u % 2][:, :]).then_inc(s_wo[u % 2], 16)
                sp.wait_ge(s_rc, g + 1)
                sp.dma_start(d["srow"].rearrange("(h n) -> h n", h=H)[:, bass.ds(g * (G * P), G * P)],
                             rows[p][:, :]).then_inc(s_ro[p], 16)
            for p in range(2):
                load(p, p)
            if NG > 2:
                with sp.Fori(0, NG // 2 - 1) as g2:
                    for p in range(2):
                        sp.wait_ge(s_tp, 2 * g2 + p + 1)
                        sp.wait_ge(s_xr, 2 * g2 + p + 1)
                        load(2 * g2 + p + 2, p)
                        store(g2, p)
            for p in range(2):
                store(NG // 2 - 1, p)
            sp.wait_ge(s_mc, 1)
            sp.dma_start(d["mean"], means[0:1, :]).then_inc(s_o, 16)
            sp.wait_ge(s_f, 3)
            sp.dma_start(d["kcol"].rearrange("h p t -> p h t"), kc[:, :, :]).then_inc(s_o, 16)
            sp.wait_ge(s_o, 32)
            for p in range(2):
                sp.wait_ge(s_wo[p], 16 * NT // 2)
                sp.wait_ge(s_ro[p], 16 * NG // 2)

        @block.tensor
        def _(pe):
            pe.wait_ge(s_id, 3)

            def group(g2, p):
                g = 2 * g2 + p
                pe.wait_ge(s_ta, g)
                pe.wait_ge(s_td, g)
                pe.wait_ge(s_x[p], 16 * (g2 + 1))
                for u in range(G):
                    for k in range(KT):
                        last = nc.tensor.transpose(ps_t[:, u, k, :], xin[p][:, u, k * P:(k + 1) * P], ident[:, :])
                last.then_inc(s_tp, 1)
                pe.wait_ge(s_wa, 1)
                pe.wait_ge(s_sc, g)
                for u in range(G):
                    t = g * G + u
                    if u == 0:
                        pe.wait_ge(s_ta, g + 1)
                    if u == G // 2:
                        pe.wait_ge(s_td, g + 1)
                    for k in range(KT):
                        nc.tensor.matmul(ps_s[:, u * 2 * H:(u + 1) * 2 * H], xt[:, u, k, :], wall[:, k, HD:],
                                         start=(k == 0), stop=(k == KT - 1))
                    pe.wait_ge(s_wc, t + 1)
                    if halves > 1:
                        pe.wait_ge(s_wd, t + 1)
                    for q in range(halves):
                        for k in range(KT):
                            last = nc.tensor.matmul(ps_w[u % 2][q][:, 0:HW], xt[:, u, k, :],
                                                    wall[:, k, q * HW:(q + 1) * HW],
                                                    start=(k == 0), stop=(k == KT - 1))
                    last.then_inc(s_mm, 1)
                pe.wait_ge(s_sc, g + 1)
                pe.wait_ge(s_rc, g)
                for u in range(G):
                    last = nc.tensor.transpose(ps_r[0:H, u * P:(u + 1) * P], scg[p][:, u, 0:H], ident[:, :])
                last.then_inc(s_rt, 1)

            with pe.Fori(0, NG // 2) as g2:
                for p in range(2):
                    group(g2, p)
            pe.wait_ge(s_f, 1)
            pe.wait_ge(s_ta, NG)
            pe.wait_ge(s_td, NG)
            for k in range(KT):
                last = nc.tensor.matmul(ps_t[:, 0, k, :], xacc[:, k * P:(k + 1) * P], ones[:, :],
                                        start=True, stop=True)
            last.then_inc(s_xm, 1)
            pe.wait_ge(s_xc, 1)
            pe.wait_ge(s_wc, NT + 2)
            if halves > 1:
                pe.wait_ge(s_wd, NT + 2)
            for q in range(halves):
                for k in range(KT):
                    last = nc.tensor.matmul(ps_w[0][q][:, 0:HW], xmean[:, k, :], wall[:, k, q * HW:(q + 1) * HW],
                                            start=(k == 0), stop=(k == KT - 1))
            last.then_inc(s_mn, 1)

        @block.scalar
        def _(act):
            act.sem_inc(s_wc, 2)

            def group(g2, p):
                g = 2 * g2 + p
                act.wait_ge(s_mm, g * G)
                act.wait_ge(s_tp, g + 1)
                act.copy(xt[:, 0:G // 2, :, :], ps_t[:, 0:G // 2, :, :]).then_inc(s_ta, 1)
                for u in range(G):
                    t = g * G + u
                    act.wait_ge(s_mm, t + 1)
                    act.wait_ge(s_wo[u % 2], 16 * (4 * g2 + 2 * p + u // 2))
                    act.copy(whs[u % 2][:, 0:HW], ps_w[u % 2][0][:, 0:HW]).then_inc(s_wc, 1)
                act.wait_ge(s_rt, g + 1)
                act.wait_ge(s_ro[p], 16 * g2)
                act.copy(rows[p][:, :], ps_r[0:H, :]).then_inc(s_rc, 1)
            with act.Fori(0, NG // 2) as g2:
                for p in range(2):
                    group(g2, p)
            act.wait_ge(s_mn, 1)
            for q in range(halves):
                last = act.copy(means[:, q * HW:(q + 1) * HW], ps_w[0][q][:, 0:HW])
            last.then_inc(s_mc, 1)
            act.wait_ge(s_f, 4)
            act.activation(facs["eu"][:, :, :], ta[:, :, :], ACT.Exp).then_inc(s_ex, 1)
            act.activation(facs["ev"][:, :, :], ta[:, :, :], ACT.Exp, scale=SLOPE).then_inc(s_ex, 1)
            act.activation(facs["sb"][:, :, :], tu[:, :, :], ACT.Exp).then_inc(s_ex, 1)
            act.activation(facs["sc"][:, :, :], tv[:, :, :], ACT.Exp).then_inc(s_ex, 1)
            act.wait_ge(s_ex, 4)

        @block.vector
        def _(dve):
            dve.sem_inc(s_wd, 2)
            ch = Chain(dve, s_ch)
            ch.link(dve.memset(xacc[:, :], 0.0))
            dve.wait_ge(s_w, 16 * (KT + 2))
            for m in range(2):
                for k in range(KT):
                    ch.link(dve.tensor_tensor(prod[:, :], wall[:, k, 0:HD], abc[:, m, :], ALU.mult))
                    ins = dve.tensor_reduce(wall[:, k, HD + m * H:HD + (m + 1) * H],
                                            prod[:, :].rearrange("p (h e) -> p h e", h=H), AX.X, ALU.add)
                    ch.link(ins)
            dve.sem_inc(s_wa, 1)
            n0, L = ch.n, 1

            def group(g2, p):
                g = 2 * g2 + p
                dve.wait_ge(s_x[p], 16 * (g2 + 1))
                dve.wait_ge(s_ch, n0 + L * g)
                dve.tensor_reduce(ext[:, bass.ds(g, 1)], xin[p][:, :, :], AX.XY, ALU.max, apply_absolute_value=True)
                dve.tensor_reduce(xpart[:, :], xin[p][:, :, :].rearrange("p g f -> p f g"), AX.X,
                                  ALU.add).then_inc(s_xr, 1)
                dve.wait_ge(s_xr, g + 1)
                dve.tensor_tensor(xacc[:, :], xacc[:, :], xpart[:, :], ALU.add).then_inc(s_ch, L)
                dve.wait_ge(s_mm, g * G)
                dve.wait_ge(s_tp, g + 1)
                dve.tensor_copy(xt[:, G // 2:, :, :], ps_t[:, G // 2:, :, :]).then_inc(s_td, 1)
                if halves > 1:
                    for u in range(G):
                        t = g * G + u
                        dve.wait_ge(s_mm, t + 1)
                        dve.wait_ge(s_wo[u % 2], 16 * (4 * g2 + 2 * p + u // 2))
                        dve.tensor_copy(whs[u % 2][:, HW:HD], ps_w[u % 2][1][:, 0:HW]).then_inc(s_wd, 1)
                dve.wait_ge(s_mm, (g + 1) * G)
                dve.wait_ge(s_rt, g)
                src = ps_s[:, 0:G * 2 * H].rearrange("p (u c) -> p u c", u=G)
                dve.tensor_copy(scg[p][:, :, :], src)
                dve.tensor_copy(scol[:, bass.ds(g * G, G), :], src).then_inc(s_sc, 1)
            with dve.Fori(0, NG // 2) as g2:
                for p in range(2):
                    group(g2, p)
            ch = Chain(dve, s_ch, n0 + L * NG)
            dve.wait_ge(s_sc, NG)
            dve.wait_ge(s_ch, n0 + L * NG)
            dve.tensor_reduce(big[:, 0:1], ext[:, :], AX.X, ALU.max)
            dve.tensor_reduce(big[:, 1:2], wall[:, :, 0:HD], AX.XY, ALU.max, apply_absolute_value=True).then_inc(s_f, 1)
            s1 = scol[:, :, 0:H].rearrange("p t h -> p h t")
            s2 = scol[:, :, H:2 * H].rearrange("p t h -> p h t")
            dve.tensor_reduce(smax[:, :], s2, AX.X, ALU.max).then_inc(s_f, 1)
            dve.tensor_scalar(kc[:, :, :], s2, STEEP, None, ALU.mult).then_inc(s_f, 1)
            dve.wait_ge(s_xm, 1)
            dve.tensor_scalar(xmean[:, :, :], ps_t[:, 0, :, :], 1.0 / N, None, ALU.mult).then_inc(s_xc, 1)
            dve.wait_ge(s_ar, 2)
            peak = smaxr[:, :].unsqueeze(2).to_broadcast([P, H, NT])
            dve.tensor_tensor(ta[:, :, :], s2, peak, ALU.subtract)
            ch.link(dve.tensor_tensor(tb[:, :, :], s1, peak, ALU.add))
            dve.tensor_scalar(tu[:, :, :], tb[:, :, :], 1.0 - SLOPE, 0.0, ALU.mult, ALU.min)
            dve.tensor_scalar(tv[:, :, :], tb[:, :, :], SLOPE - 1.0, 0.0, ALU.mult, ALU.min).then_inc(s_f, 1)
            ch.link(dve.tensor_tensor(lam[:, 0:1], bigr[:, 0:1], bigr[:, 1:2], ALU.mult))
            ch.link(dve.tensor_scalar(lam[:, 1:2], lam[:, 0:1], float(F), 1.0, ALU.mult, ALU.max))
            ch.link(dve.reciprocal(lam[:, 2:3], lam[:, 1:2]))
            ch.link(dve.tensor_scalar(lam[:, 3:4], lam[:, 2:3], 2.0 ** 15, None, ALU.mult))
            dve.wait_ge(s_ex, 4)
            for name in ("eu", "ev"):
                ch.link(dve.tensor_scalar(facs[name][:, :, :], facs[name][:, :, :], lam[:, 3:4], None, ALU.mult))


def attention_phase(nc, tag, mask_t, d, facs, N, H, D, out, elu):
    NT, NB = N // P, N // BLK
    JC = NT // CPB
    W1 = D + 1
    CW = BLK // 4
    G = H * NB
    HC = CPB * NB
    assert NB % 2 == 0 and H % 2 == 0
    with ExitStack() as ctx:
        s = Scope(nc, ctx, tag)
        uv = s.sb("uv", [P, (CPB + 2) * JC, 4 * W1], F16)
        bbuf = [s.sb(f"b{k}", [P, JC, BLK], F8) for k in range(NBUF)]
        cbuf = [s.sb(f"c{k}", [P, JC, BLK], F8) for k in range(NBUF)]
        s1b = [s.sb(f"s1b{q}", [P, BLK], F32) for q in range(2)]
        kcur = [s.sb(f"kcur{q}", [P, NT], F32) for q in range(2)]
        mnb = [s.sb(f"mnb{q}", [P, D], F32) for q in range(2)]
        whx = [s.sb(f"whx{k}", [P, JC, W1], F32) for k in range(4)]
        tu = s.sb("tu", [P, JC, W1], F32)
        tv = s.sb("tv", [P, JC, W1], F32)
        e1 = [s.sb(f"e1{q}", [P, 2 * W1], F32) for q in range(2)]
        nt = [s.sb(f"nt{q}", [P, W1], F32) for q in range(2)]
        mt = [s.sb(f"mt{q}", [P, D], F32) for q in range(2)]
        sm = [s.sb(f"sm{q}", [P, 4], F32) for q in range(2)]
        ob = [s.sb(f"ob{t}", [P, D], F32) for t in range(TPB)]
        ps = [[s.ps(f"ps{t}{m}", [P, BANK]) for m in range(2)] for t in range(TPB)]
        s_pad = s.sem("pad")
        s_blk = [s.sem(f"blk{q}") for q in range(2)]
        s_wh = [s.sem(f"wh{k}") for k in range(4)]
        s_one = s.sem("one")
        s_uv = s.sem("uv")
        s_pl = s.sem("pl")
        s_cmp = s.sem("cmp")
        s_bc = s.sem("bc")
        s_pe = s.sem("pe")
        s_mm = s.sem("mm")
        s_e1 = s.sem("e1")
        s_ev = s.sem("ev")
        s_dv = s.sem("dv")
        s_m, s_ex = s.sem("m"), s.sem("ex")
        s_out = s.sem("out")
        s_st = [s.sem(f"st{t}") for t in range(TPB)]
        block = ctx.enter_context(nc.Block())

        def slot(par, c):
            return (CPB + c if par and c < 2 else c) * JC

        @block.gpsimd
        def _(pool):
            for k in range(4):
                ins = nc.gpsimd.memset(whx[k][:, :, :], 1.0)
                ins.then_inc(s_one, 1)
            L = 5

            def make(hp, par):
                h = 2 * hp + par
                for m, c in enumerate(MAKE):
                    n = h * CPB + m
                    k = m % 4
                    pool.wait_ge(s_wh[k], 16 * (2 * h + m // 4 + 1))
                    pool.wait_ge(s_uv, n)
                    fac = lambda f: facs[f][:, :, :].rearrange("p h t -> p (h t)")[
                        :, bass.ds(h * NT + c * JC, JC)].unsqueeze(2).to_broadcast([P, JC, W1])
                    nc.gpsimd.tensor_tensor(tu[:, :, :], whx[k][:, :, :], fac("eu"), ALU.mult)
                    nc.gpsimd.tensor_tensor(tv[:, :, :], whx[k][:, :, :], fac("ev"), ALU.mult).then_inc(s_pl, 1)
                    pool.wait_ge(s_pl, 2 * n + 1)
                    pool.wait_ge(s_pe, PE_OFFSET + HC * h - (HC if c < 2 else c))
                    held(pool, s_pad)
                    at = lambda j: uv[:, slot(par, c):slot(par, c) + JC, j * W1:(j + 1) * W1]
                    nc.gpsimd.tensor_copy(at(0), tu[:, :, :])
                    nc.gpsimd.tensor_copy(at(2), tv[:, :, :]).then_inc(s_pl, 1)
                    pool.wait_ge(s_pl, 2 * n + 2)
                    nc.gpsimd.tensor_tensor(at(1), tu[:, :, :], at(0), ALU.subtract)
                    nc.gpsimd.tensor_tensor(at(3), tv[:, :, :], at(2), ALU.subtract).then_inc(s_uv, 1)
            with pool.Fori(0, H // 2) as hp:
                for par in range(2):
                    make(hp, par)

        @block.sync
        def _(sp):
            srow = d["srow"].unsqueeze(0)
            kcol = d["kcol"].rearrange("h p t -> p h t")
            mean = d["mean"]
            whv = d["wh"].rearrange("(t p) c -> p t c", p=P)

            def load_block(h, b, q):
                sp.dma_start(s1b[q][:, :], srow[0:1, bass.ds(h * N + b * BLK, BLK)].to_broadcast([P, BLK])
                             ).then_inc(s_blk[q], 16)
                sp.dma_start(kcur[q][:, :], kcol[:, bass.ds(h, 1), :].rearrange("p a t -> p (a t)")
                             ).then_inc(s_blk[q], 16)
                sp.dma_start(mnb[q][:, :], mean[0:1, bass.ds(h * D, D)].to_broadcast([P, D])).then_inc(s_blk[q], 16)

            def load_wh(h, m):
                c, k = MAKE[m], m % 4
                sp.dma_start(whx[k][:, :, 0:D], whv[:, c * JC:(c + 1) * JC, bass.ds(h * D, D)]).then_inc(s_wh[k], 16)

            def head(h, last):
                for b in range(NB):
                    g = h * NB + b
                    if not (last and b == NB - 1):
                        sp.wait_ge(s_cmp, CPB * g)
                        held(sp, s_pad)
                        sp.wait_ge(s_out, TPB * g)
                        nb = (b + 1) % NB
                        load_block(h + 1 if nb == 0 else h, nb, nb % 2)
                    if b == NB - 1 and not last:
                        for m in range(4, 8):
                            sp.wait_ge(s_uv, (h + 1) * CPB + m - 3)
                            load_wh(h + 1, m)
                    for t in range(TPB):
                        sp.wait_ge(s_out, TPB * g + t + 1)
                        sp.dma_start(out[bass.ds(b * BLK + t * P, P), bass.ds(h * D, D)],
                                     ob[t][:, :]).then_inc(s_st[t], 16)
                    if b == 0 and not last:
                        for m in range(4):
                            sp.wait_ge(s_uv, h * CPB + 4 + m + 1)
                            load_wh(h + 1, m)
            sp.wait_ge(s_one, 4)
            load_block(0, 0, 0)
            for m in range(4):
                load_wh(0, m)
            for m in range(4, 8):
                sp.wait_ge(s_uv, m - 3)
                load_wh(0, m)
            with sp.Fori(0, H - 1) as h:
                head(h, False)
            head(H - 1, True)
            for t in range(TPB):
                sp.wait_ge(s_st[t], 16 * G)

        @block.tensor
        def _(pe):
            def sweep(hp, par, b2, q):
                h = 2 * hp + par
                g = h * NB + 2 * b2 + q
                order = SWEEP[q]
                groups = [(0, 1)] + [(k,) for k in range(2, CPB - 2)] + [(CPB - 2, CPB - 1)]
                for ks in groups:
                    pe.wait_ge(s_bc, CPB * g + ks[-1] + 1)
                    pe.wait_ge(s_uv, CPB * h + 1 + max(MAKE.index(order[k]) for k in ks))
                    held(pe, s_pad)
                    for t in range(TPB):
                        if ks[0] == 0:
                            pe.wait_ge(s_ev, TPB * g + t + 1)
                            held(pe, s_pad)
                        for k in ks:
                            for j in range(JC):
                                first = ks[0] == 0 and k == 0 and j == 0
                                end = k == CPB - 1 and j == JC - 1
                                row = uv[:, slot(par, order[k]) + j, :]
                                for m, buf in enumerate((bbuf, cbuf)):
                                    last = nc.tensor.matmul(ps[t][m][:, 0:2 * W1],
                                                            buf[k % NBUF][:, j, t * P:(t + 1) * P],
                                                            row[:, 2 * m * W1:2 * (m + 1) * W1],
                                                            start=first, stop=end)
                        if ks[-1] == CPB - 1 and t < TPB - 1:
                            last.then_inc(s_mm, 1)
                    last.then_inc(s_pe, len(ks))
            with pe.Fori(0, H // 2) as hp:
                for par in range(2):
                    with pe.Fori(0, NB // 2) as b2:
                        for q in range(2):
                            sweep(hp, par, b2, q)

        @block.scalar
        def _(act):
            act.sem_inc(s_pe, PE_OFFSET)

            def compare(g, q, k, q_wait):
                act.wait_ge(s_pe, CPB * g + (PE_OFFSET + k + 1 - NBUF))
                if k == 0:
                    act.wait_ge(s_blk[q], q_wait)
                held(act, s_pad)
                for j in range(JC):
                    jt = SWEEP[q][k] * JC + j
                    last = act.activation(bbuf[k % NBUF][:, j, :], s1b[q][:, :], ACT.Relu,
                                          bias=kcur[q][:, jt:jt + 1], scale=STEEP, saturate=False)
                last.then_inc(s_cmp, 1)

            def body(g2, last):
                for q in range(2):
                    g = 2 * g2 + q
                    for k in range(2, CPB):
                        compare(g, q, k, None)
                    if not (last and q == 1):
                        for k in range(2):
                            compare(g + 1, 1 - q, k, 48 * (g2 + 1 + q))
                    def scale(t):
                        if t < TPB - 1:
                            act.wait_ge(s_mm, (TPB - 1) * g + t + 1)
                        else:
                            act.wait_ge(s_pe, CPB * g + (PE_OFFSET + CPB))
                        act.wait_ge(s_ev, TPB * g + t + (TPB - 1))
                        act.mul(e1[t % 2][:, :], ps[t][0][:, 0:2 * W1],
                                facs["sb"][:, :, :].rearrange("p h t -> p (h t)")[:, bass.ds(g * TPB + t, 1)]
                                ).then_inc(s_e1, 1)

                    def exp(t):
                        act.wait_ge(s_m, TPB * g + t + 1)
                        act.activation(mt[t % 2][:, :], mt[t % 2][:, :], ACT.Exp).then_inc(s_ex, 1)
                    scale(0)
                    scale(1)
                    for t in range(TPB):
                        if elu:
                            exp(t)
                        if t + 2 < TPB:
                            scale(t + 2)
            for k in range(2):
                compare(0, 0, k, 48)
            with act.Fori(0, G // 2 - 1) as g2:
                body(g2, False)
            body(G // 2 - 1, True)

        @block.vector
        def _(dve):
            dve.sem_inc(s_ev, TPB)
            links = 5 if elu else 2

            def split(g, q, b, k):
                jt = SWEEP[q][k] * JC
                m = mask_t[:, :, :].bitcast(U32)[:, jt:jt + JC, bass.ds(b * CW, CW)]
                x = bbuf[k % NBUF][:, :, :].bitcast(U32)
                dve.wait_ge(s_cmp, CPB * g + k + 1)
                dve.scalar_tensor_tensor(cbuf[k % NBUF][:, :, :].bitcast(U32), x, ONE8X4, m,
                                         ALU.bitwise_xor, ALU.bitwise_and)
                dve.tensor_tensor(x, x, m, ALU.bitwise_and).then_inc(s_bc, 1)

            def body(g2, last):
                for q in range(2):
                    g = 2 * g2 + q
                    b, bn = (2 * g2) % NB + q, (2 * g2 + q + 1) % NB
                    for k in range(2, CPB):
                        split(g, q, b, k)
                    if not (last and q == 1):
                        for k in range(2):
                            split(g + 1, 1 - q, bn, k)

                    def finish(t):
                        n = TPB * g + t
                        ch = Chain(dve, s_dv, n * links)
                        e, v, z = e1[t % 2], nt[t % 2], sm[t % 2]
                        fac = facs["sc"][:, :, :].rearrange("p h t -> p (h t)")[:, bass.ds(n, 1)]
                        dve.wait_ge(s_e1, n + 1)
                        ch.link(dve.scalar_tensor_tensor(e[:, :], ps[t][1][:, 0:2 * W1], fac, e[:, :],
                                                         ALU.mult, ALU.add))
                        dve.tensor_tensor(v[:, :], e[:, 0:W1], e[:, W1:2 * W1], ALU.add).then_inc(s_ev, 1)
                        dve.wait_ge(s_ev, n + (TPB + 1))
                        if elu:
                            ch.link(dve.tensor_scalar(z[:, 0:1], v[:, D:W1], 0.0, None, ALU.is_equal))
                            dve.tensor_tensor(z[:, 1:2], v[:, D:W1], z[:, 0:1], ALU.add)
                            ch.link(dve.scalar_tensor_tensor(v[:, 0:D], mnb[q][:, :], z[:, 0:1], v[:, 0:D],
                                                             ALU.mult, ALU.add))
                            ch.link(dve.reciprocal(z[:, 2:3], z[:, 1:2]))
                            dve.tensor_scalar(mt[t % 2][:, :], v[:, 0:D], z[:, 2:3], 0.0,
                                              ALU.mult, ALU.min).then_inc(s_m, 1)
                            ch.mark(dve.tensor_scalar(v[:, 0:D], v[:, 0:D], z[:, 2:3], 0.0, ALU.mult, ALU.max))
                        else:
                            ch.link(dve.reciprocal(z[:, 2:3], v[:, D:W1]))
                            dve.wait_ge(s_st[t], 16 * g)
                            dve.tensor_scalar(ob[t][:, :], v[:, 0:D], z[:, 2:3], None, ALU.mult).then_inc(s_out, 1)

                    def add_exp(t):
                        n = TPB * g + t
                        dve.wait_ge(s_ex, n + 1)
                        dve.wait_ge(s_dv, (n + 1) * links)
                        dve.wait_ge(s_st[t], 16 * g)
                        dve.scalar_tensor_tensor(ob[t][:, :], mt[t % 2][:, :], -1.0, nt[t % 2][:, 0:D],
                                                 ALU.add, ALU.add).then_inc(s_out, 1)
                    for t in range(TPB):
                        finish(t)
                        if elu and t > 0:
                            add_exp(t - 1)
                    if elu:
                        add_exp(TPB - 1)
            for k in range(2):
                split(0, 0, 0, k)
            with dve.Fori(0, G // 2 - 1) as g2:
                body(g2, False)
            body(G // 2 - 1, True)


def norm_tile(dve, ch, z, st, s_v, s_r, it, s_stored, i2, ob, s_o, s_pad):
    ch.link(dve.bn_stats(st[:, 0:6], z[:, :]))
    held(dve, s_pad)
    ch.link(dve.bn_aggr(st[:, 6:8], st[:, 0:6]))
    dve.tensor_scalar(st[:, 8:9], st[:, 7:8], LN_EPS, None, ALU.add).then_inc(s_v, 1)
    dve.wait_ge(s_r, it + 1)
    ch.link(dve.reciprocal(st[:, 9:10], st[:, 8:9]))
    dve.wait_ge(s_stored, 16 * i2)
    dve.tensor_scalar(ob[:, :], z[:, :], st[:, 6:7], st[:, 9:10], ALU.subtract, ALU.mult).then_inc(s_o, 1)


def project_phase(nc, feat, W_out, b_out, x, out):
    N, K = feat.shape
    F = W_out.shape[1]
    NT, KT = N // P, K // P
    KB = KT // 2
    with ExitStack() as ctx:
        s = Scope(nc, ctx, "pj")
        wo = s.sb("wo", [P, KT, F], F32)
        bb = s.sb("bb", [P, F], F32)
        ident = s.sb("ident", [P, P], F32)
        fin = [s.sb(f"fin{p}", [P, K], F32) for p in range(2)]
        xin = [s.sb(f"xin{p}", [P, F], F32) for p in range(2)]
        ft = [s.sb(f"ft{p}", [P, KT, P], F32) for p in range(2)]
        z = [s.sb(f"z{p}", [P, F], F32) for p in range(2)]
        st = [s.sb(f"st{p}", [P, 10], F32) for p in range(2)]
        ob = [s.sb(f"ob{p}", [P, F], F32) for p in range(2)]
        ps_t = [[s.ps(f"pt{p}{m}", [P, KB, P]) for m in range(2)] for p in range(2)]
        ps_y = [s.ps(f"py{p}", [P, BANK]) for p in range(2)]
        s_w, s_id = s.sem("w"), s.sem("id")
        s_ld = [s.sem(f"ld{p}") for p in range(2)]
        s_tp = s.sem("tp")
        s_ta, s_td = s.sem("ta"), s.sem("td")
        s_y = s.sem("y")
        s_z = s.sem("z")
        s_ch = s.sem("ch")
        s_v, s_r = s.sem("v"), s.sem("r")
        s_o = s.sem("o")
        s_pad = s.sem("pad")
        s_st = [s.sem(f"st{p}") for p in range(2)]
        block = ctx.enter_context(nc.Block())

        @block.gpsimd
        def _(pool):
            make_identity(nc, pool, ident, s_id)

        @block.sync
        def _(sp):
            sp.dma_start(wo[:, :, :], W_out.rearrange("(k p) f -> p k f", p=P)).then_inc(s_w, 16)
            sp.dma_start(bb[:, :], b_out.unsqueeze(0).to_broadcast([P, F])).then_inc(s_w, 16)

            def load(it, p):
                sp.dma_start(fin[p][:, :], feat[bass.ds(it * P, P), :]).then_inc(s_ld[p], 16)
                sp.dma_start(xin[p][:, :], x[bass.ds(it * P, P), :]).then_inc(s_ld[p], 16)

            def store(it, p):
                sp.wait_ge(s_o, it + 1)
                sp.dma_start(out[bass.ds(it * P, P), :], ob[p][:, :]).then_inc(s_st[p], 16)
            for p in range(2):
                load(p, p)
            with sp.Fori(0, NT // 2 - 1) as i2:
                for p in range(2):
                    sp.wait_ge(s_tp, 2 * i2 + p + 1)
                    sp.wait_ge(s_z, 2 * i2 + p + 1)
                    load(2 * i2 + p + 2, p)
                    store(2 * i2 + p, p)
            for p in range(2):
                store(NT - 2 + p, p)
            for p in range(2):
                sp.wait_ge(s_st[p], 16 * NT // 2)

        @block.tensor
        def _(pe):
            pe.wait_ge(s_id, 2)
            pe.wait_ge(s_w, 32)

            def turn(i2, p):
                it = 2 * i2 + p
                pe.wait_ge(s_ld[p], 32 * (i2 + 1))
                pe.wait_ge(s_ta, 2 * i2)
                pe.wait_ge(s_td, 2 * i2)
                for k in range(KT):
                    last = nc.tensor.transpose(ps_t[p][k // KB][:, k % KB, :], fin[p][:, k * P:(k + 1) * P],
                                               ident[:, :])
                last.then_inc(s_tp, 1)

            def multiply(i2, p):
                it = 2 * i2 + p
                pe.wait_ge(s_ta, it + 1)
                pe.wait_ge(s_td, it + 1)
                pe.wait_ge(s_z, 2 * i2)
                for k in range(KT):
                    last = nc.tensor.matmul(ps_y[p][:, 0:F], ft[p][:, k, :], wo[:, k, :],
                                            start=(k == 0), stop=(k == KT - 1))
                last.then_inc(s_y, 1)
            turn(0, 0)
            with pe.Fori(0, NT // 2 - 1) as i2:
                turn(i2, 1)
                multiply(i2, 0)
                turn(i2 + 1, 0)
                multiply(i2, 1)
            turn(NT // 2 - 1, 1)
            multiply(NT // 2 - 1, 0)
            multiply(NT // 2 - 1, 1)

        @block.scalar
        def _(act):
            def body(i2, p):
                it = 2 * i2 + p
                act.wait_ge(s_y, 2 * i2)
                act.wait_ge(s_tp, it + 1)
                act.copy(ft[p][:, 0:KB, :], ps_t[p][0][:, :, :]).then_inc(s_ta, 1)

            def root(it, p):
                act.wait_ge(s_v, it + 1)
                act.activation(st[p][:, 8:9], st[p][:, 8:9], ACT.Sqrt).then_inc(s_r, 1)
            body(0, 0)
            with act.Fori(0, NT // 2 - 1) as i2:
                body(i2, 1)
                root(2 * i2, 0)
                body(i2 + 1, 0)
                root(2 * i2 + 1, 1)
            body(NT // 2 - 1, 1)
            root(NT - 2, 0)
            root(NT - 1, 1)

        @block.vector
        def _(dve):
            dve.wait_ge(s_w, 32)

            def body(i2, p):
                it = 2 * i2 + p
                dve.wait_ge(s_y, 2 * i2)
                dve.wait_ge(s_tp, it + 1)
                dve.tensor_copy(ft[p][:, KB:, :], ps_t[p][1][:, :, :]).then_inc(s_td, 1)

            links = 4

            def norm(i2, p):
                it = 2 * i2 + p
                ch = Chain(dve, s_ch, it * links)
                dve.wait_ge(s_ld[p], 32 * (i2 + 1))
                ch.link(dve.tensor_tensor(xin[p][:, :], xin[p][:, :], bb[:, :], ALU.add))
                dve.wait_ge(s_y, it + 1)
                dve.tensor_tensor(z[p][:, :], ps_y[p][:, 0:F], xin[p][:, :], ALU.add).then_inc(s_z, 1)
                dve.wait_ge(s_z, it + 1)

                norm_tile(dve, ch, z[p], st[p], s_v, s_r, it, s_st[p], i2, ob[p], s_o, s_pad)
            body(0, 0)
            with dve.Fori(0, NT // 2 - 1) as i2:
                body(i2, 1)
                norm(i2, 0)
                body(i2 + 1, 0)
                norm(i2, 1)
            body(NT // 2 - 1, 1)
            norm(NT // 2 - 1, 0)
            norm(NT // 2 - 1, 1)


def final_phase(nc, h, x, out):
    N, F = x.shape
    NT = N // P
    with ExitStack() as ctx:
        s = Scope(nc, ctx, "fn")
        hin = [s.sb(f"hin{p}", [P, F], F32) for p in range(2)]
        xin = [s.sb(f"xin{p}", [P, F], F32) for p in range(2)]
        z = [s.sb(f"z{p}", [P, F], F32) for p in range(2)]
        st = [s.sb(f"st{p}", [P, 10], F32) for p in range(2)]
        ob = [s.sb(f"ob{p}", [P, F], F32) for p in range(2)]
        s_ld = [s.sem(f"ld{p}") for p in range(2)]
        s_z, s_ch, s_v, s_r, s_o, s_pad = (s.sem(n) for n in ("z", "ch", "v", "r", "o", "pad"))
        s_st = [s.sem(f"st{p}") for p in range(2)]
        block = ctx.enter_context(nc.Block())

        @block.sync
        def _(sp):
            def load(it, p):
                sp.dma_start(hin[p][:, :], h[bass.ds(it * P, P), :]).then_inc(s_ld[p], 16)
                sp.dma_start(xin[p][:, :], x[bass.ds(it * P, P), :]).then_inc(s_ld[p], 16)

            def store(it, p):
                sp.wait_ge(s_o, it + 1)
                sp.dma_start(out[bass.ds(it * P, P), :], ob[p][:, :]).then_inc(s_st[p], 16)
            for p in range(2):
                load(p, p)
            with sp.Fori(0, NT // 2 - 1) as i2:
                for p in range(2):
                    sp.wait_ge(s_z, 2 * i2 + p + 1)
                    load(2 * i2 + p + 2, p)
                    store(2 * i2 + p, p)
            for p in range(2):
                store(NT - 2 + p, p)
            for p in range(2):
                sp.wait_ge(s_st[p], 16 * NT // 2)

        @block.scalar
        def _(act):
            with act.Fori(0, NT // 2) as i2:
                for p in range(2):
                    act.wait_ge(s_v, 2 * i2 + p + 1)
                    act.activation(st[p][:, 8:9], st[p][:, 8:9], ACT.Sqrt).then_inc(s_r, 1)

        @block.vector
        def _(dve):
            with dve.Fori(0, NT // 2) as i2:
                for p in range(2):
                    it = 2 * i2 + p
                    ch = Chain(dve, s_ch, it * 3)
                    dve.wait_ge(s_ld[p], 32 * (i2 + 1))
                    dve.tensor_tensor(z[p][:, :], hin[p][:, :], xin[p][:, :], ALU.add).then_inc(s_z, 1)
                    dve.wait_ge(s_z, it + 1)
                    norm_tile(dve, ch, z[p], st[p], s_v, s_r, it, s_st[p], i2, ob[p], s_o, s_pad)


def program(nc, x, adj, W0, a1, a2, W_out, b_out, W1, a_pair, out):
    N, F = x.shape
    H0, _, D0 = W0.shape
    H1, _, D1 = W1.shape
    NT = N // P
    dram = lambda name, *shape: nc.dram_tensor(name, shape, F32).ap()
    feat, x1, h1 = dram("feat", N, H0 * D0), dram("x1", N, F), dram("h1", N, H1 * D1)
    with ExitStack() as ctx:
        mask_t = ctx.enter_context(nc.sbuf_tensor("mask_t", [P, NT, N], U8))
        mask_phase(nc, adj, mask_t)
        for tag, xs, W, pair, H, D, dst in (("l0", x, W0, (a1, a2), H0, D0, feat),
                                            ("l1", x1, W1, (a_pair[:, 0:D1], a_pair[:, D1:]), H1, D1, h1)):
            d = {"wh": dram(tag + "_wh", N, H * D), "srow": dram(tag + "_srow", H * N),
                 "kcol": dram(tag + "_kcol", H, P, NT), "mean": dram(tag + "_mean", 1, H * D)}
            with ExitStack() as inner:
                facs = {n: inner.enter_context(nc.sbuf_tensor(f"{tag}_{n}", [P, H, NT], F32))
                        for n in ("eu", "ev", "sb", "sc")}
                prep_phase(nc, tag + "p", xs, W, pair[0], pair[1], d, facs)
                attention_phase(nc, tag + "a", mask_t, d, facs, N, H, D, dst, elu=tag == "l0")
            if tag == "l0":
                project_phase(nc, feat, W_out, b_out, x, x1)
    final_phase(nc, h1, x1, out)


_INS = ["x", "adj", "L0_gnn_W_heads", "L0_gnn_a1", "L0_gnn_a2", "L0_gnn_W_out", "L0_gnn_b_out", "L1_gnn_W", "L1_gnn_a"]


def kernel(**inputs):
    import concourse.bacc as bacc
    from concourse.bass_utils import run_bass_kernel_spmd

    nc = bacc.Bacc("TRN2", target_bir_lowering=False, num_devices=1, dynamic_dma_scratch_size=1024)
    arrays, aps = {}, []
    for name in _INS:
        a = np.ascontiguousarray(inputs[name])
        arrays["in_" + name] = a
        aps.append(nc.dram_tensor("in_" + name, a.shape, mybir.dt.from_np(a.dtype), kind="ExternalInput").ap())
    out = nc.dram_tensor("out_0", inputs["x"].shape, F32, kind="ExternalOutput").ap()
    program(nc, *aps, out)
    return run_bass_kernel_spmd(nc, [arrays], core_ids=[0]).results[0]["out_0"]
```

```python
from contextlib import ExitStack

import numpy as np

import concourse.bass as bass
from concourse import mybir

P = 128
F32 = mybir.dt.float32
F16 = mybir.dt.float16
BF16 = mybir.dt.bfloat16
F8 = mybir.dt.float8e4
I32 = mybir.dt.int32
U32 = mybir.dt.uint32
U8 = mybir.dt.uint8
ALU = mybir.AluOpType
ACT = mybir.ActivationFunctionType
AX = mybir.AxisListType
ABSMAX = bass.bass_isa.ReduceOp.absmax
RMAX = bass.bass_isa.ReduceOp.max

BANK = 512
BLK = 512
TPB = BLK // P
CPB = 8
SLOPE = 0.2
STEEP = 2.0 ** 64
ONE8 = 0x38
ONE8X4 = 0x38383838
LN_EPS = 1e-5
SWEEP = [list(range(CPB)), list(range(CPB))[::-1]]
MAKE = [0, 1, 7, 6, 2, 3, 4, 5]
PLANS = {"l0": dict(dve_tiles=0, nbuf=4, ahead=2), "l1": dict(dve_tiles=1, nbuf=8, ahead=4)}
PE_OFFSET = 1024
GT = 4


class Scope:

    def __init__(self, nc, ctx, tag):
        self.nc, self.ctx, self.tag = nc, ctx, tag

    def sb(self, name, shape, dt):
        return self.ctx.enter_context(self.nc.sbuf_tensor(f"{self.tag}_{name}", shape, dt))

    def ps(self, name, shape, dt=F32):
        return self.ctx.enter_context(self.nc.psum_tensor(f"{self.tag}_{name}", shape, dt))

    def sem(self, name):
        return self.ctx.enter_context(self.nc.semaphore(f"{self.tag}_{name}"))


class Chain:

    def __init__(self, eng, sem, base=0):
        self.eng, self.sem, self.base, self.n = eng, sem, base, 0

    def mark(self, ins):
        ins.then_inc(self.sem, 1)
        self.n += 1
        return self.base + self.n

    def wait(self, value):
        self.eng.wait_ge(self.sem, value)

    def link(self, ins):
        self.wait(self.mark(ins))


def held(eng, pad):
    eng.sem_inc(pad, 1)


def make_identity(nc, pool, tile, sem):
    nc.gpsimd.memset(tile[:, :], 1.0).then_inc(sem, 1)
    pool.wait_ge(sem, 1)
    nc.gpsimd.affine_select(out=tile[:, :], in_=tile[:, :], compare_op=ALU.is_equal, fill=0.0, base=0,
                            pattern=[[-1, P]], channel_multiplier=1).then_inc(sem, 1)


def prep_phase(nc, tag, x, W, a1, a2, d, facs, adj=None, mask_t=None):
    N, F = x.shape
    H, _, D = W.shape
    HD, NT, KT = H * D, N // P, F // P
    G = GT
    NG = NT // G
    halves = max(1, HD // BANK)
    HW = HD // halves
    Q = 4
    QW = N // Q
    QT = QW // P
    mean = "mean" in d
    joined = halves == 1 and HD + 2 * H <= BANK
    with ExitStack() as ctx:
        s = Scope(nc, ctx, tag)
        wall = s.sb("wall", [P, KT, HD + 2 * H], F32)
        abc = s.sb("abc", [P, 2, HD], F32)
        prod = s.sb("prod", [P, HD], F32)
        xin = [s.sb(f"xin{u}", [P, F], F32) for u in range(G)]
        xt = [s.sb(f"xt{p}", [P, KT, P], F32) for p in range(2)]
        whs = [s.sb(f"whs{p}", [P, HD], F32) for p in range(2)]
        scg = s.sb("scg", [P, G, 2 * H], F32)
        scol = s.sb("scol", [P, NT, 2 * H], F32)
        rows = s.sb("rows", [H, G * P], F32)
        ident = s.sb("ident", [P, P], F32)
        ones = s.sb("ones", [P, P], F32)
        xacc = s.sb("xacc", [P, F], F32)
        xmean = s.sb("xmean", [P, KT, P], F32)
        means = s.sb("means", [P, HD], F32)
        ext = s.sb("ext", [P, NT], F32)
        big = s.sb("big", [P, 2], F32)
        bigr = s.sb("bigr", [P, 2], F32)
        lam = s.sb("lam", [P, 4], F32)
        smax = s.sb("smax", [P, H], F32)
        smaxr = s.sb("smaxr", [P, H], F32)
        ta, tb, tu, tv, kc, nk = (s.sb(n, [P, H, NT], F32) for n in ("ta", "tb", "tu", "tv", "kc", "nk"))
        ps_t = s.ps("pst", [P, KT, P])
        wsets = 2 if joined else 1
        ps_w = [s.ps(f"psw{q}", [P, BANK]) for q in range(halves * wsets)]
        ps_s = s.ps("pss", [P, BANK])
        s_w = s.sem("w")
        s_id = s.sem("id")
        s_wa = s.sem("wa")
        s_xl = [s.sem(f"xl{u}") for u in range(G)]
        s_tp, s_tc = s.sem("tp"), s.sem("tc")
        s_pw = [s.sem(f"pw{q}") for q in range(halves)]
        s_cw = [s.sem(f"cw{q}") for q in range(halves)]
        s_s, s_sc = s.sem("s"), s.sem("sc")
        s_rt, s_rc = s.sem("rt"), s.sem("rc")
        s_xr = s.sem("xr")
        s_wo = [s.sem(f"wo{p}") for p in range(2)]
        s_ro = s.sem("ro")
        s_ch = s.sem("ch")
        s_f = s.sem("f")
        s_ar = s.sem("ar")
        s_ex = s.sem("ex")
        s_xm, s_xc, s_mn, s_mc = (s.sem(n) for n in ("xm", "xc", "mn", "mc"))
        s_o = s.sem("o")
        s_pad = s.sem("pad")
        if adj is not None:
            raw = [s.sb(f"raw{r}", [P, QW], I32) for r in range(Q)]
            bits = [s.sb(f"bits{r}", [P, QW], BF16) for r in range(Q)]
            ident16 = s.sb("ident16", [P, P], BF16)
            ps_m = [s.ps(f"psm{r}", [P, QT, P], BF16) for r in range(Q)]
            s_rl = [s.sem(f"rl{r}") for r in range(Q)]
            s_cv = s.sem("cv")
            s_mt = s.sem("mt")
            s_ma, s_md = s.sem("ma"), s.sem("md")
        block = ctx.enter_context(nc.Block())

        def quarter(r, t):
            return mask_t[:, r * QT:(r + 1) * QT, bass.ds(t * P, P)]

        def groups(eng, body):
            with eng.Fori(0, NG - 1) as g:
                body(g, False)
            body(NG - 1, True)

        @block.gpsimd
        def _(pool):
            make_identity(nc, pool, ident, s_id)
            nc.gpsimd.memset(ones[:, :], 1.0).then_inc(s_id, 1)
            if adj is not None:
                pool.wait_ge(s_id, 2)
                nc.gpsimd.tensor_copy(ident16[:, :], ident[:, :]).then_inc(s_id, 1)
            pool.wait_ge(s_f, 1)
            nc.gpsimd.partition_all_reduce(bigr[:, :], big[:, :], P, ABSMAX).then_inc(s_ar, 1)
            pool.wait_ge(s_f, 2)
            nc.gpsimd.partition_all_reduce(smaxr[:, :], smax[:, :], P, RMAX).then_inc(s_ar, 1)

        @block.sync
        def _(sp):
            for p in range(2):
                sp.sem_inc(s_wo[p], 16)
            sp.sem_inc(s_ro, 16)

            def load_x(t, u):
                sp.dma_start(xin[u][:, :], x[bass.ds(t * P, P), :]).then_inc(s_xl[u], 16)

            def load_row(t, r):
                sp.dma_start(raw[r][:, :], adj[bass.ds(t * P, P), r * QW:(r + 1) * QW]).then_inc(s_rl[r], 16)
            load_x(0, 0)
            if adj is not None:
                for r in range(Q):
                    load_row(0, r)
            for k in range(KT):
                sp.dma_start(wall[:, k, 0:HD].rearrange("p (h e) -> p h e", h=H),
                             W[:, k * P:(k + 1) * P, :].rearrange("h p e -> p h e")).then_inc(s_w, 16)
            for m, a in enumerate((a1, a2)):
                sp.dma_start(abc[:, m, :].rearrange("p (h e) -> p h e", h=H),
                             a.unsqueeze(0).to_broadcast([P, H, D])).then_inc(s_w, 16)
            for u in range(1, G):
                load_x(u, u)
            if adj is not None:
                for r in range(Q):
                    sp.wait_ge(s_cv, r + 1)
                    load_row(1, r)

            def group(g, last):
                for u in range(G):
                    t = g * G + u
                    if adj is not None and not (last and u >= G - 2):
                        for r in range(Q):
                            sp.wait_ge(s_cv, Q * t + (Q + r + 1))
                            held(sp, s_pad)
                            load_row(t + 2, r)
                    for q in range(halves):
                        sp.wait_ge(s_cw[q], t + 1 + wsets)
                        held(sp, s_pad)
                    sp.dma_start(d["wh"][bass.ds(t * P, P), :], whs[u % 2][:, :]).then_inc(s_wo[u % 2], 16)
                    if not last:
                        sp.wait_ge(s_xr, t + 2)
                        held(sp, s_pad)
                        load_x(t + G, u)
                sp.wait_ge(s_rc, g + 2)
                held(sp, s_pad)
                sp.dma_start(d["srow"].rearrange("(h n) -> h n", h=H)[:, bass.ds(g * (G * P), G * P)],
                             rows[:, :]).then_inc(s_ro, 16)
            groups(sp, group)
            sp.wait_ge(s_f, 3)
            sp.dma_start(d["kcol"].rearrange("h p t -> p h t"), kc[:, :, :]).then_inc(s_o, 16)
            sp.dma_start(d["ncol"].rearrange("h p t -> p h t"), nk[:, :, :]).then_inc(s_o, 16)
            if mean:
                sp.wait_ge(s_mc, 1)
                sp.dma_start(d["mean"], means[0:1, :]).then_inc(s_o, 16)
            sp.wait_ge(s_o, 48 if mean else 32)
            for p in range(2):
                sp.wait_ge(s_wo[p], 16 * (NT // 2 + 1))
            sp.wait_ge(s_ro, 16 * (NG + 1))

        @block.tensor
        def _(pe):
            pe.wait_ge(s_id, 3 if adj is None else 4)

            def turn(loads, u):
                pe.wait_ge(s_xl[u], loads)
                for k in range(KT):
                    last = nc.tensor.transpose(ps_t[:, k, :], xin[u][:, k * P:(k + 1) * P], ident[:, :])
                last.then_inc(s_tp, 1)

            def product(t, u, q):
                pe.wait_ge(s_cw[q], t + 1)
                bank = ps_w[u % 2 if joined else q]
                cols = slice(0, HD + 2 * H) if joined else slice(q * HW, (q + 1) * HW)
                for k in range(KT):
                    last = nc.tensor.matmul(bank[:, 0:cols.stop - cols.start], xt[u % 2][:, k, :],
                                            wall[:, k, cols], start=(k == 0), stop=(k == KT - 1))
                last.then_inc(s_pw[q], 1)

            def turn_mask(t, r):
                pe.wait_ge(s_cv, Q * t + (r + 1))
                if r < Q - 1:
                    pe.wait_ge(s_ma, (Q - 1) * t + (r + 1))
                else:
                    pe.wait_ge(s_md, t + 1)
                for m in range(QT):
                    last = nc.tensor.transpose(ps_m[r][:, m, :], bits[r][:, m * P:(m + 1) * P], ident16[:, :])
                last.then_inc(s_mt, 1)

            def group(g, last):
                for u in range(G):
                    t = g * G + u
                    pe.wait_ge(s_tc, t + 1)
                    more = not (last and u == G - 1)
                    if joined and more:
                        turn(16 * (g + (u + 1) // G + 1), (u + 1) % G)
                    product(t, u, 0)
                    if adj is not None:
                        turn_mask(t, 0)
                        turn_mask(t, 1)
                    if more and not joined:
                        turn(16 * (g + (u + 1) // G + 1), (u + 1) % G)
                    if halves > 1:
                        product(t, u, 1)
                    if u == 0:
                        pe.wait_ge(s_rc, g + 1)
                        if not joined:
                            pe.wait_ge(s_wa, 1)
                    if not joined:
                        for k in range(KT):
                            ins = nc.tensor.matmul(ps_s[:, u * 2 * H:(u + 1) * 2 * H], xt[u % 2][:, k, :],
                                                   wall[:, k, HD:], start=(k == 0), stop=(k == KT - 1))
                        if u == G - 1:
                            ins.then_inc(s_s, 1)
                    if adj is not None:
                        turn_mask(t, 2)
                        turn_mask(t, 3)
                pe.wait_ge(s_sc, g + 1)
                for u in range(G):
                    ins = nc.tensor.transpose(ps_s[0:H, u * P:(u + 1) * P], scg[:, u, 0:H], ident[:, :])
                ins.then_inc(s_rt, 1)

            pe.wait_ge(s_w, 16 * (KT + 2))
            turn(16, 0)
            if joined:
                pe.wait_ge(s_wa, 1)
            groups(pe, group)
            if not mean:
                return
            pe.wait_ge(s_xr, NT + 1)
            for k in range(KT):
                last = nc.tensor.matmul(ps_t[:, k, :], xacc[:, k * P:(k + 1) * P], ones[:, :], start=True, stop=True)
            last.then_inc(s_xm, 1)
            pe.wait_ge(s_xc, 1)
            for q in range(halves):
                pe.wait_ge(s_cw[q], NT + 1)
                for k in range(KT):
                    last = nc.tensor.matmul(ps_w[q][:, 0:HW], xmean[:, k, :], wall[:, k, q * HW:(q + 1) * HW],
                                            start=(k == 0), stop=(k == KT - 1))
            last.then_inc(s_mn, 1)

        @block.scalar
        def _(act):
            if halves > 1:
                act.sem_inc(s_cw[0], wsets)
            act.sem_inc(s_rc, 1)
            if adj is not None:
                act.sem_inc(s_ma, Q - 1)

            def copy_x(t, p):
                act.wait_ge(s_tp, t + 1)
                act.copy(xt[p][:, :, :], ps_t[:, :, :]).then_inc(s_tc, 1)

            def write_mask(t, r):
                act.wait_ge(s_mt, Q * t + (r + 1))
                act.copy(quarter(r, t), ps_m[r][:, :, :]).then_inc(s_ma, 1)

            def group(g, last):
                for u in range(G):
                    t = g * G + u
                    if halves > 1:
                        act.wait_ge(s_wo[u % 2], 16 * (2 * g + u // 2 + 1))
                        act.wait_ge(s_pw[0], t + 1)
                        act.copy(whs[u % 2][:, 0:HW], ps_w[0][:, 0:HW]).then_inc(s_cw[0], 1)
                    if adj is not None:
                        write_mask(t, 0)
                        write_mask(t, 1)
                    if not (last and u == G - 1):
                        copy_x(t + 1, (u + 1) % 2)
                    if adj is not None:
                        write_mask(t, 2)
                act.wait_ge(s_ro, 16 * (g + 1))
                act.wait_ge(s_rt, g + 1)
                act.copy(rows[:, :], ps_s[0:H, :]).then_inc(s_rc, 1)
            copy_x(0, 0)
            groups(act, group)
            act.wait_ge(s_f, 4)
            act.activation(facs["eu"][:, :, :], ta[:, :, :], ACT.Exp).then_inc(s_ex, 1)
            act.activation(facs["ev"][:, :, :], ta[:, :, :], ACT.Exp, scale=SLOPE).then_inc(s_ex, 1)
            act.activation(facs["sb"][:, :, :], tu[:, :, :], ACT.Exp).then_inc(s_ex, 1)
            act.activation(facs["sc"][:, :, :], tv[:, :, :], ACT.Exp).then_inc(s_ex, 1)
            if mean:
                act.wait_ge(s_mn, 1)
                for q in range(halves):
                    last = act.copy(means[:, q * HW:(q + 1) * HW], ps_w[q][:, 0:HW])
                last.then_inc(s_mc, 1)
            act.wait_ge(s_ex, 4)

        @block.vector
        def _(dve):
            dve.sem_inc(s_cw[-1], wsets)
            dve.sem_inc(s_xr, 1)
            if adj is not None:
                dve.sem_inc(s_md, 1)

            def compare(t, r, first=False):
                dve.wait_ge(s_rl[r], 16 * (t + 1))
                if not first:
                    dve.wait_ge(s_mt, Q * t + (r + 1 - Q))
                dve.tensor_scalar(bits[r][:, :], raw[r][:, :], 0.0, float(ONE8), ALU.is_gt,
                                  ALU.mult).then_inc(s_cv, 1)
            if adj is not None:
                for r in range(Q):
                    compare(0, r, True)
            ch = Chain(dve, s_ch)
            ch.link(dve.memset(xacc[:, :], 0.0))
            dve.wait_ge(s_w, 16 * (KT + 2))
            for m in range(2):
                for k in range(KT):
                    ch.link(dve.tensor_tensor(prod[:, :], wall[:, k, 0:HD], abc[:, m, :], ALU.mult))
                    ch.link(dve.tensor_reduce(wall[:, k, HD + m * H:HD + (m + 1) * H],
                                              prod[:, :].rearrange("p (h e) -> p h e", h=H), AX.X, ALU.add))
            dve.sem_inc(s_wa, 1)
            dve.tensor_reduce(big[:, 1:2], wall[:, :, 0:HD], AX.XY, ALU.max, apply_absolute_value=True)

            def group(g, last):
                for u in range(G):
                    t = g * G + u
                    more = adj is not None and not (last and u == G - 1)
                    if more:
                        compare(t + 1, 0)
                        compare(t + 1, 1)
                    dve.wait_ge(s_wo[u % 2], 16 * (2 * g + u // 2 + 1))
                    dve.wait_ge(s_pw[-1], t + 1)
                    bank = ps_w[u % 2 if joined else halves - 1]
                    copied = dve.tensor_copy(whs[u % 2][:, HD - HW:HD], bank[:, 0:HW])
                    if joined:
                        if u == 0:
                            dve.wait_ge(s_rc, g + 1)
                        dve.tensor_copy(scg[:, u, :], bank[:, HD:HD + 2 * H])
                        copied = dve.tensor_copy(scol[:, bass.ds(t, 1), :].rearrange("p a c -> p (a c)"),
                                                 bank[:, HD:HD + 2 * H])
                    copied.then_inc(s_cw[-1], 1)
                    if joined and u == G - 1:
                        dve.wait_ge(s_cw[-1], t + 1 + wsets)
                        dve.sem_inc(s_sc, 1)
                    elif u == G - 1:
                        dve.wait_ge(s_s, g + 1)
                        src = ps_s[:, 0:G * 2 * H].rearrange("p (u c) -> p u c", u=G)
                        dve.tensor_copy(scg[:, :, :], src)
                        dve.tensor_copy(scol[:, bass.ds(g * G, G), :], src).then_inc(s_sc, 1)
                    if more:
                        compare(t + 1, 2)
                    if adj is not None:
                        dve.wait_ge(s_mt, Q * t + Q)
                        dve.tensor_copy(quarter(Q - 1, t), ps_m[Q - 1][:, :, :]).then_inc(s_md, 1)
                    if more:
                        compare(t + 1, 3)
                    dve.wait_ge(s_xl[u], 16 * (g + 1))
                    dve.wait_ge(s_tp, t + 1)
                    ins = dve.tensor_reduce(ext[:, bass.ds(t, 1)], xin[u][:, :], AX.X, ALU.max,
                                            apply_absolute_value=True)
                    if mean:
                        dve.wait_ge(s_xr, t + 1)
                        ins = dve.tensor_tensor(xacc[:, :], xacc[:, :], xin[u][:, :], ALU.add)
                    ins.then_inc(s_xr, 1)
            groups(dve, group)
            dve.wait_ge(s_sc, NG)
            dve.wait_ge(s_xr, NT + 1)
            dve.tensor_reduce(big[:, 0:1], ext[:, :], AX.X, ALU.max).then_inc(s_f, 1)
            s1 = scol[:, :, 0:H].rearrange("p t h -> p h t")
            s2 = scol[:, :, H:2 * H].rearrange("p t h -> p h t")
            dve.tensor_reduce(smax[:, :], s2, AX.X, ALU.max).then_inc(s_f, 1)
            dve.tensor_scalar(kc[:, :, :], s2, STEEP, None, ALU.mult)
            dve.tensor_scalar(nk[:, :, :], s2, -1.0, None, ALU.mult).then_inc(s_f, 1)
            if mean:
                dve.wait_ge(s_xm, 1)
                dve.tensor_scalar(xmean[:, :, :], ps_t[:, :, :], 1.0 / N, None, ALU.mult).then_inc(s_xc, 1)
            dve.wait_ge(s_ar, 2)
            peak = smaxr[:, :].unsqueeze(2).to_broadcast([P, H, NT])
            dve.tensor_tensor(ta[:, :, :], s2, peak, ALU.subtract)
            ch.link(dve.tensor_tensor(tb[:, :, :], s1, peak, ALU.add))
            dve.tensor_scalar(tu[:, :, :], tb[:, :, :], 1.0 - SLOPE, 0.0, ALU.mult, ALU.min)
            dve.tensor_scalar(tv[:, :, :], tb[:, :, :], SLOPE - 1.0, 0.0, ALU.mult, ALU.min).then_inc(s_f, 1)
            ch.link(dve.tensor_tensor(lam[:, 0:1], bigr[:, 0:1], bigr[:, 1:2], ALU.mult))
            ch.link(dve.tensor_scalar(lam[:, 1:2], lam[:, 0:1], float(F), 1.0, ALU.mult, ALU.max))
            ch.link(dve.reciprocal(lam[:, 2:3], lam[:, 1:2]))
            ch.link(dve.tensor_scalar(lam[:, 3:4], lam[:, 2:3], 2.0 ** 15, None, ALU.mult))
            dve.wait_ge(s_ex, 4)
            for name in ("eu", "ev"):
                ch.link(dve.tensor_scalar(facs[name][:, :, :], facs[name][:, :, :], lam[:, 3:4], None, ALU.mult))


def attention_phase(nc, tag, mask_t, d, facs, N, H, D, out, elu, dve_tiles, nbuf, ahead):
    NT, NB = N // P, N // BLK
    JC = NT // CPB
    W1 = D + 1
    CW = BLK // 4
    G = H * NB
    HC = CPB * NB
    links = TPB + (TPB + 3 if elu else 1)
    sets = 1 if 4 * W1 > BANK else 2
    LOADS = 16 * (2 + (dve_tiles > 0) + elu)
    assert NB % 2 == 0 and H % 2 == 0
    with ExitStack() as ctx:
        s = Scope(nc, ctx, tag)
        uv = s.sb("uv", [P, (CPB + 2) * JC, 4 * W1], F16)
        bbuf = [s.sb(f"b{k}", [P, JC, BLK], F8) for k in range(nbuf)]
        cbuf = [s.sb(f"c{k}", [P, JC, BLK], F8) for k in range(nbuf)]
        s1b = [s.sb(f"s1b{q}", [P, BLK], F32) for q in range(2)]
        kcur = [s.sb(f"kcur{q}", [P, NT], F32) for q in range(2)]
        ncur = [s.sb(f"ncur{q}", [P, NT], F32) for q in range(2)]
        mnb = [s.sb(f"mnb{q}", [P, D], F32) for q in range(2)]
        whx = [s.sb(f"whx{k}", [P, JC, W1], F32) for k in range(4)]
        tu = s.sb("tu", [P, JC, W1], F32)
        tv = s.sb("tv", [P, JC, W1], F32)
        e1 = [s.sb(f"e1{t}", [P, 2 * W1], F32) for t in range(TPB)]
        vt = s.sb("vt", [P, TPB, W1], F32)
        mt = s.sb("mt", [P, TPB, D], F32)
        zr = s.sb("zr", [P, 3, TPB], F32)
        ob = s.sb("ob", [P, TPB, D], F32)
        ps = [[s.ps(f"ps{t}{m}", [P, BANK]) for m in range(2)] for t in range(TPB)]
        if sets == 2:
            zeros = s.sb("zeros", [P, 4 * W1], F16)
        s_pad = s.sem("pad")
        s_blk = [s.sem(f"blk{q}") for q in range(2)]
        s_wh = [s.sem(f"wh{k}") for k in range(4)]
        s_one = s.sem("one")
        s_uv = s.sem("uv")
        s_pl = s.sem("pl")
        s_ud = s.sem("ud")
        s_ca, s_cd = s.sem("ca"), s.sem("cd")
        s_bc = s.sem("bc")
        s_pe = s.sem("pe")
        s_mm = s.sem("mm")
        s_e1 = s.sem("e1")
        s_ev = s.sem("ev")
        s_dv = s.sem("dv")
        s_m, s_ex = s.sem("m"), s.sem("ex")
        s_out = s.sem("out")
        s_st = s.sem("st")
        block = ctx.enter_context(nc.Block())

        def sums(q, t, m):
            return ps[t][m][:, 0:2 * W1] if sets == 1 else ps[t][q][:, m * 2 * W1:(m + 1) * 2 * W1]

        def slot(par, c):
            return (CPB + c if par and c < 2 else c) * JC

        def part(par, c, j):
            return uv[:, slot(par, c):slot(par, c) + JC, j * W1:(j + 1) * W1]

        def factor(name, h, c):
            return column(name, h * NT + c * JC, JC).unsqueeze(2).to_broadcast([P, JC, W1])

        def column(name, at, n=1):
            return facs[name][:, :, :].rearrange("p h t -> p (h t)")[:, bass.ds(at, n)]

        @block.gpsimd
        def _(pool):
            pool.sem_inc(s_uv, 1)
            if sets == 2:
                nc.gpsimd.memset(zeros[:, :], 0.0).then_inc(s_one, 1)
            for k in range(4):
                nc.gpsimd.memset(whx[k][:, :, :], 1.0).then_inc(s_one, 1)

            def make(hp, par, shared=False):
                h = 2 * hp + par
                parts = ((tv, "ev", 2),) if shared else ((tu, "eu", 0), (tv, "ev", 2))
                for m in range(CPB):
                    n = h * CPB + m
                    k, c = m % 4, MAKE[m]
                    pool.wait_ge(s_wh[k], 16 * (2 * h + m // 4 + 1))
                    pool.wait_ge(s_uv, n + 1)
                    pool.wait_ge(s_pe, PE_OFFSET + HC * h - (HC if c < 2 else c))
                    for t, f, j in parts:
                        nc.gpsimd.tensor_tensor(t[:, :, :], whx[k][:, :, :], factor(f, h, c), ALU.mult)
                        last = nc.gpsimd.tensor_tensor(part(par, c, j), whx[k][:, :, :], factor(f, h, c), ALU.mult)
                    last.then_inc(s_pl, 1)
                    pool.wait_ge(s_pl, n + 1)
                    if shared:
                        pool.wait_ge(s_ud, 2 * m + 2)
                    for t, f, j in parts:
                        last = nc.gpsimd.tensor_tensor(part(par, c, j + 1), t[:, :, :], part(par, c, j), ALU.subtract)
                    last.then_inc(s_uv, 1)
            make(0, 0, True)
            make(0, 1)
            with pool.Fori(1, H // 2) as hp:
                for par in range(2):
                    make(hp, par)

        @block.sync
        def _(sp):
            srow = d["srow"].unsqueeze(0)
            whv = d["wh"].rearrange("(t p) c -> p t c", p=P)
            outv = out.rearrange("(t p) c -> p t c", p=P)

            def load_block(h, b, q):
                sp.dma_start(s1b[q][:, :], srow[0:1, bass.ds(h * N + b * BLK, BLK)].to_broadcast([P, BLK])
                             ).then_inc(s_blk[q], 16)
                for tile, name in ((kcur, "kcol"), (ncur, "ncol"))[:2 if dve_tiles else 1]:
                    sp.dma_start(tile[q][:, :], d[name].rearrange("h p t -> p h t")[:, bass.ds(h, 1), :].rearrange(
                        "p a t -> p (a t)")).then_inc(s_blk[q], 16)
                if elu:
                    sp.dma_start(mnb[q][:, :], d["mean"][0:1, bass.ds(h * D, D)].to_broadcast([P, D])
                                 ).then_inc(s_blk[q], 16)

            def load_wh(h, m):
                c, k = MAKE[m], m % 4
                sp.dma_start(whx[k][:, :, 0:D], whv[:, c * JC:(c + 1) * JC, bass.ds(h * D, D)]).then_inc(s_wh[k], 16)

            def head(h, last):
                for b in range(NB):
                    g = h * NB + b
                    if not (last and b == NB - 1):
                        sp.wait_ge(s_out, g + 1)
                        nb = (b + 1) % NB
                        load_block(h + 1 if nb == 0 else h, nb, nb % 2)
                    if b == NB - 1 and not last:
                        for m in range(4, 8):
                            sp.wait_ge(s_uv, (h + 1) * CPB + m - 2)
                            load_wh(h + 1, m)
                    sp.wait_ge(s_out, g + 2)
                    sp.dma_start(outv[:, b * TPB:(b + 1) * TPB, bass.ds(h * D, D)], ob[:, :, :]).then_inc(s_st, 16)
                    if b == 0 and not last:
                        for m in range(4):
                            sp.wait_ge(s_uv, h * CPB + 4 + m + 2)
                            load_wh(h + 1, m)
            sp.wait_ge(s_one, 3 + sets)
            load_block(0, 0, 0)
            for m in range(4):
                load_wh(0, m)
            for m in range(4, 8):
                sp.wait_ge(s_uv, m - 2)
                load_wh(0, m)
            with sp.Fori(0, H - 1) as h:
                head(h, False)
            head(H - 1, True)
            sp.wait_ge(s_st, 16 * (G + 1))

        @block.tensor
        def _(pe):
            def sweep(hp, par, b2, q):
                h = 2 * hp + par
                g = h * NB + 2 * b2 + q
                order = SWEEP[q]
                groups = [(0, 1)] + [(k,) for k in range(2, CPB - 2)] + [(CPB - 2, CPB - 1)]
                for ks in groups:
                    pe.wait_ge(s_bc, CPB * g + ks[-1] + 1)
                    pe.wait_ge(s_uv, CPB * h + 2 + max(MAKE.index(order[k]) for k in ks))
                    held(pe, s_pad)
                    for t in range(TPB):
                        if ks[0] == 0:
                            pe.wait_ge(s_ev, TPB * g + t + 1)
                            held(pe, s_pad)
                            if sets == 2:
                                nc.tensor.matmul(ps[t][q][:, 0:4 * W1], zeros[:, 0:P], zeros[:, :],
                                                 start=True, stop=False)
                        for k in ks:
                            for j in range(JC):
                                first = ks[0] == 0 and k == 0 and j == 0
                                end = k == CPB - 1 and j == JC - 1
                                row = uv[:, slot(par, order[k]) + j, :]
                                for m, buf in enumerate((bbuf, cbuf)):
                                    last = nc.tensor.matmul(sums(q, t, m),
                                                            buf[k % nbuf][:, j, t * P:(t + 1) * P],
                                                            row[:, 2 * m * W1:2 * (m + 1) * W1],
                                                            start=first and sets == 1,
                                                            stop=end and m >= sets - 1)
                        if ks[-1] == CPB - 1 and t < TPB - 1:
                            last.then_inc(s_mm, 1)
                    last.then_inc(s_pe, len(ks))
            pe.wait_ge(s_one, 3 + sets)
            with pe.Fori(0, H // 2) as hp:
                for par in range(2):
                    with pe.Fori(0, NB // 2) as b2:
                        for q in range(2):
                            sweep(hp, par, b2, q)

        def blocks(eng, body):
            for q in range(2):
                body(0, q, q == 0, False)
            with eng.Fori(1, G // 2 - 1) as g2:
                for q in range(2):
                    body(g2, q, False, False)
            for q in range(2):
                body(G // 2 - 1, q, False, q == 1)

        @block.scalar
        def _(act):
            act.sem_inc(s_pe, PE_OFFSET)

            def compare(g, q, k, loads=None):
                act.wait_ge(s_pe, CPB * g + (PE_OFFSET + k + 1 - nbuf))
                if k == 0:
                    act.wait_ge(s_blk[q], loads)
                held(act, s_pad)
                for j in range(JC - dve_tiles):
                    jt = SWEEP[q][k] * JC + j
                    last = act.activation(bbuf[k % nbuf][:, j, :], s1b[q][:, :], ACT.Relu,
                                          bias=kcur[q][:, jt:jt + 1], scale=STEEP, saturate=False)
                last.then_inc(s_ca, 1)

            def exponentials(g):
                act.wait_ge(s_m, g)
                act.activation(mt[:, :, :], mt[:, :, :], ACT.Exp).then_inc(s_ex, 1)

            def body(g2, q, first, last):
                g = 2 * g2 + q
                compare(g, q, ahead)
                if elu and not first:
                    exponentials(g)
                for k in range(ahead + 1, CPB):
                    compare(g, q, k)
                if not last:
                    for k in range(ahead):
                        compare(g + 1, 1 - q, k, LOADS * (g2 + 1 + q))
                for t in range(TPB):
                    if t < TPB - 1:
                        act.wait_ge(s_mm, (TPB - 1) * g + t + 1)
                    else:
                        act.wait_ge(s_pe, CPB * g + (PE_OFFSET + CPB))
                    act.wait_ge(s_dv, g * links + t + 1)
                    act.mul(e1[t][:, :], sums(q, t, 0), column("sb", g * TPB + t)).then_inc(s_e1, 1)
                if elu and last:
                    exponentials(g + 1)
            for k in range(ahead):
                compare(0, 0, k, LOADS)
            blocks(act, body)

        @block.vector
        def _(dve):
            dve.sem_inc(s_ev, TPB * sets)
            dve.sem_inc(s_out, 1)
            dve.sem_inc(s_st, 16)
            dve.sem_inc(s_dv, links)

            def compare(g, q, k, loads=None):
                if dve_tiles:
                    dve.wait_ge(s_pe, CPB * g + (PE_OFFSET + k + 1 - nbuf))
                    if k == 0:
                        dve.wait_ge(s_blk[q], loads)
                    held(dve, s_pad)
                    for j in range(JC - dve_tiles, JC):
                        jt = SWEEP[q][k] * JC + j
                        ins = dve.tensor_scalar(bbuf[k % nbuf][:, j, :], s1b[q][:, :], ncur[q][:, jt:jt + 1], None,
                                                ALU.is_gt, saturate=False)
                    ins.then_inc(s_cd, 1)

            def make(m):
                k, c = m % 4, MAKE[m]
                dve.wait_ge(s_wh[k], 16 * (m // 4 + 1))
                if m > 0:
                    dve.wait_ge(s_ud, 2 * m)
                dve.tensor_tensor(tu[:, :, :], whx[k][:, :, :], factor("eu", 0, c), ALU.mult)
                dve.tensor_tensor(part(0, c, 0), whx[k][:, :, :], factor("eu", 0, c), ALU.mult).then_inc(s_ud, 1)
                dve.wait_ge(s_ud, 2 * m + 1)
                dve.tensor_tensor(part(0, c, 1), tu[:, :, :], part(0, c, 0), ALU.subtract).then_inc(s_ud, 1)

            def split(g, q, b, k):
                jt = SWEEP[q][k] * JC
                m = mask_t[:, :, :].bitcast(U32)[:, jt:jt + JC, bass.ds(b * CW, CW)]
                x = bbuf[k % nbuf][:, :, :].bitcast(U32)
                if dve_tiles:
                    dve.wait_ge(s_cd, CPB * g + (k + 1))
                dve.wait_ge(s_ca, CPB * g + (k + 1))
                dve.scalar_tensor_tensor(cbuf[k % nbuf][:, :, :].bitcast(U32), x, ONE8X4, m,
                                         ALU.bitwise_xor, ALU.bitwise_and)
                dve.tensor_tensor(x, x, m, ALU.bitwise_and).then_inc(s_bc, 1)

            def evacuate(g, q):
                def fold(t):
                    dve.wait_ge(s_ev, TPB * (g + sets) + t + 1)
                    dve.tensor_tensor(vt[:, t, :], e1[t][:, 0:W1], e1[t][:, W1:2 * W1], ALU.add).then_inc(s_dv, 1)
                for t in range(TPB):
                    n = TPB * g + t
                    dve.wait_ge(s_e1, n + 1)
                    dve.scalar_tensor_tensor(e1[t][:, :], sums(q, t, 1), column("sc", n), e1[t][:, :],
                                             ALU.mult, ALU.add).then_inc(s_ev, 1)
                    if t > 0:
                        fold(t - 1)
                fold(TPB - 1)

            def divide(g, q):
                dve.wait_ge(s_dv, (g + 1) * links + TPB)
                ch = Chain(dve, s_dv, (g + 1) * links + TPB)
                den = vt[:, :, D:W1].rearrange("p t a -> p (t a)")
                if not elu:
                    ch.link(dve.reciprocal(zr[:, 2, :], den))
                    dve.wait_ge(s_st, 16 * (g + 1))
                    dve.tensor_tensor(ob[:, :, :], vt[:, :, 0:D], zr[:, 2, :].unsqueeze(2).to_broadcast([P, TPB, D]),
                                      ALU.mult).then_inc(s_out, 1)
                    return
                ch.link(dve.tensor_scalar(zr[:, 0, :], den, 0.0, None, ALU.is_equal))
                ch.mark(dve.tensor_tensor(zr[:, 1, :], den, zr[:, 0, :], ALU.add))
                for t in range(TPB):
                    v = vt[:, t, 0:D]
                    ins = dve.scalar_tensor_tensor(v, mnb[q][:, :], zr[:, 0, t:t + 1], v, ALU.mult, ALU.add)
                    if t < TPB - 1:
                        ch.mark(ins)
                    if t == 0:
                        ch.wait((g + 1) * links + TPB + 2)
                        dve.reciprocal(zr[:, 2, :], zr[:, 1, :])
                ch.link(ins)
                for t in range(TPB):
                    ins = dve.tensor_scalar(mt[:, t, :], vt[:, t, 0:D], zr[:, 2, t:t + 1], 0.0, ALU.mult, ALU.min)
                ins.then_inc(s_m, 1)
                for t in range(TPB):
                    v = vt[:, t, 0:D]
                    ins = dve.tensor_scalar(v, v, zr[:, 2, t:t + 1], 0.0, ALU.mult, ALU.max)
                ch.mark(ins)

            def add_exponentials(g):
                dve.wait_ge(s_ex, g)
                dve.wait_ge(s_dv, (g + 1) * links)
                dve.wait_ge(s_st, 16 * g)
                dve.scalar_tensor_tensor(ob[:, :, :], mt[:, :, :], -1.0, vt[:, :, 0:D],
                                         ALU.add, ALU.add).then_inc(s_out, 1)

            def body(g2, q, first, last):
                g = 2 * g2 + q
                b, bn = (2 * g2) % NB + q, (2 * g2 + q + 1) % NB
                turns = [(0, k) for k in range(ahead, CPB)] + ([] if last else [(1, k) for k in range(ahead)])
                for m, (nxt, k) in enumerate(turns):
                    if m + 1 < len(turns):
                        nxt2, k2 = turns[m + 1]
                        compare(g + nxt2, q ^ nxt2, k2, LOADS * (g2 + 1 + q))
                    elif not last:
                        compare(g + 1, 1 - q, ahead)
                    if first and not nxt:
                        make(k)
                    split(g + nxt, q ^ nxt, bn if nxt else b, k)
                    if m == 0 and elu and not first:
                        add_exponentials(g)
                evacuate(g, q)
                divide(g, q)
                if elu and last:
                    add_exponentials(g + 1)
            compare(0, 0, 0, LOADS)
            for k in range(ahead):
                compare(0, 0, k + 1)
                make(k)
                split(0, 0, 0, k)
            blocks(dve, body)


class Norm:

    def __init__(self, s, F):
        self.z = s.sb("z", [P, GT, F], F32)
        self.st = s.sb("st", [P, GT, 6], F32)
        self.mv = s.sb("mv", [P, GT, 2], F32)
        self.rt = s.sb("rt", [P, GT], F32)
        self.rs = s.sb("rs", [P, GT], F32)
        self.warm = s.sb("warm", [P, 1], F32)
        self.s_v, self.s_r = s.sem("v"), s.sem("r")
        self.s_n = s.sem("n")
        self.s_wm = s.sem("wm")
        self.s_pad = s.sem("pad")

    LINKS = 2 * GT + 1

    def fill(self, dve):
        dve.memset(self.warm[:, :], 1.0).then_inc(self.s_wm, 1)

    def warm_up(self, act):
        act.wait_ge(self.s_wm, 1)
        act.activation(self.warm[:, :], self.warm[:, :], ACT.Sqrt)

    def stats(self, dve, g, tiles):
        ch = Chain(dve, self.s_n, g * self.LINKS + 2 * tiles[0])
        for u in tiles:
            made = ch.mark(dve.bn_stats(self.st[:, u, :], self.z[:, u, :]))
        ch.wait(made)
        held(dve, self.s_pad)
        for u in tiles:
            made = ch.mark(dve.bn_aggr(self.mv[:, u, :], self.st[:, u, :]))
        if u == GT - 1:
            ch.wait(made)
            dve.tensor_scalar(self.rt[:, :], self.mv[:, :, 1:2].rearrange("p u a -> p (u a)"), LN_EPS, None,
                              ALU.add).then_inc(self.s_v, 1)

    def root(self, act, g):
        act.wait_ge(self.s_v, g + 1)
        act.activation(self.rt[:, :], self.rt[:, :], ACT.Sqrt).then_inc(self.s_r, 1)

    def apply(self, dve, g, out):
        dve.wait_ge(self.s_r, g + 1)
        Chain(dve, self.s_n, g * self.LINKS + 2 * GT).link(dve.reciprocal(self.rs[:, :], self.rt[:, :]))
        for u in range(GT):
            last = dve.tensor_scalar(out[:, u, :], self.z[:, u, :], self.mv[:, u, 0:1], self.rs[:, u:u + 1],
                                     ALU.subtract, ALU.mult)
        return last


def project_phase(nc, feat, W_out, b_out, x, out):
    N, K = feat.shape
    F = W_out.shape[1]
    NT, KT = N // P, K // P
    NG = NT // GT
    KB = KT // 2
    with ExitStack() as ctx:
        s = Scope(nc, ctx, "pj")
        norm = Norm(s, F)
        wo = s.sb("wo", [P, KT, F], F32)
        bb = s.sb("bb", [P, F], F32)
        ident = s.sb("ident", [P, P], F32)
        fin = [s.sb(f"fin{u}", [P, K], F32) for u in range(GT)]
        xin = [s.sb(f"xin{u}", [P, F], F32) for u in range(GT)]
        ft = [s.sb(f"ft{p}", [P, KT, P], F32) for p in range(2)]
        ob = s.sb("ob", [P, GT, F], F32)
        ps_t = [[s.ps(f"pt{p}{m}", [P, KB, P]) for m in range(2)] for p in range(2)]
        ps_y = [s.ps(f"py{p}", [P, BANK]) for p in range(2)]
        s_w, s_id = s.sem("w"), s.sem("id")
        s_fl = [s.sem(f"fl{u}") for u in range(GT)]
        s_xl = [s.sem(f"xl{u}") for u in range(GT)]
        s_xb = s.sem("xb")
        s_tp = s.sem("tp")
        s_ta, s_td = s.sem("ta"), s.sem("td")
        s_y = s.sem("y")
        s_z = s.sem("z_")
        s_o = s.sem("o")
        s_st = s.sem("st_")
        block = ctx.enter_context(nc.Block())

        def groups(eng, body):
            with eng.Fori(0, NG - 1) as g:
                body(g, False)
            body(NG - 1, True)

        @block.gpsimd
        def _(pool):
            make_identity(nc, pool, ident, s_id)
            pool.wait_ge(s_w, 32)

            def group(g, last):
                for u in range(GT):
                    pool.wait_ge(s_xl[u], 16 * (g + 1))
                    nc.gpsimd.tensor_tensor(xin[u][:, :], xin[u][:, :], bb[:, :], ALU.add).then_inc(s_xb, 1)
            groups(pool, group)

        @block.sync
        def _(sp):
            def load_feat(g, u):
                sp.dma_start(fin[u][:, :], feat[bass.ds((GT * g + u) * P, P), :]).then_inc(s_fl[u], 16)

            def load_x(g, u):
                sp.dma_start(xin[u][:, :], x[bass.ds((GT * g + u) * P, P), :]).then_inc(s_xl[u], 16)
            load_feat(0, 0)
            sp.dma_start(wo[:, :, :], W_out.rearrange("(k p) f -> p k f", p=P)).then_inc(s_w, 16)
            sp.dma_start(bb[:, :], b_out.unsqueeze(0).to_broadcast([P, F])).then_inc(s_w, 16)
            for u in range(1, GT):
                load_feat(0, u)
            for u in range(GT):
                load_x(0, u)
            outv = out.rearrange("(t p) f -> p t f", p=P)

            def group(g, last):
                for u in range(GT):
                    t = GT * g + u
                    if not last:
                        sp.wait_ge(s_tp, t + 1)
                        load_feat(g + 1, u)
                        if u > 0:
                            sp.wait_ge(s_z, t + 2)
                            load_x(g + 1, u - 1)
                if not last:
                    sp.wait_ge(s_z, GT * g + (GT + 2))
                    load_x(g + 1, GT - 1)
                sp.wait_ge(s_o, g + 1)
                sp.dma_start(outv[:, bass.ds(GT * g, GT), :], ob[:, :, :]).then_inc(s_st, 16)
            groups(sp, group)
            sp.wait_ge(s_st, 16 * (NG + 1))

        @block.tensor
        def _(pe):
            pe.wait_ge(s_id, 2)
            pe.sem_inc(s_y, 2)

            def turn(g, u):
                t = GT * g + u
                pe.wait_ge(s_fl[u], 16 * (g + 1))
                pe.wait_ge(s_ta, t + 1)
                pe.wait_ge(s_td, t + 1)
                for k in range(KT):
                    last = nc.tensor.transpose(ps_t[u % 2][k // KB][:, k % KB, :], fin[u][:, k * P:(k + 1) * P],
                                               ident[:, :])
                last.then_inc(s_tp, 1)

            def multiply(g, u):
                t = GT * g + u
                pe.wait_ge(s_ta, t + 3)
                pe.wait_ge(s_td, t + 3)
                pe.wait_ge(s_z, t + 1)
                for k in range(KT):
                    last = nc.tensor.matmul(ps_y[u % 2][:, 0:F], ft[u % 2][:, k, :], wo[:, k, :],
                                            start=(k == 0), stop=(k == KT - 1))
                last.then_inc(s_y, 1)

            def group(g, last):
                for u in range(GT):
                    if not (last and u == GT - 1):
                        turn(g + (u + 1) // GT, (u + 1) % GT)
                    multiply(g, u)
            turn(0, 0)
            pe.wait_ge(s_w, 32)
            groups(pe, group)

        @block.scalar
        def _(act):
            norm.warm_up(act)
            act.sem_inc(s_ta, 2)

            def copy_feat(g, u):
                t = GT * g + u
                act.wait_ge(s_y, t + 1)
                act.wait_ge(s_tp, t + 1)
                act.copy(ft[u % 2][:, 0:KB, :], ps_t[u % 2][0][:, :, :]).then_inc(s_ta, 1)

            def group(g, last):
                for u in range(GT):
                    if not (last and u == GT - 1):
                        copy_feat(g + (u + 1) // GT, (u + 1) % GT)
                norm.root(act, g)
            copy_feat(0, 0)
            groups(act, group)

        @block.vector
        def _(dve):
            norm.fill(dve)
            dve.sem_inc(s_td, 2)
            dve.sem_inc(s_z, 2)
            dve.sem_inc(s_st, 16)

            def copy_feat(g, u):
                t = GT * g + u
                dve.wait_ge(s_y, t + 1)
                dve.wait_ge(s_tp, t + 1)
                dve.tensor_copy(ft[u % 2][:, KB:, :], ps_t[u % 2][1][:, :, :]).then_inc(s_td, 1)

            def add(g, u):
                t = GT * g + u
                dve.wait_ge(s_xb, t + 1)
                dve.wait_ge(s_y, t + 3)
                dve.tensor_tensor(norm.z[:, u, :], ps_y[u % 2][:, 0:F], xin[u][:, :], ALU.add).then_inc(s_z, 1)
                dve.wait_ge(s_z, t + 3)
                norm.stats(dve, g, [u])

            def group(g, last):
                for u in range(GT):
                    if not (last and u == GT - 1):
                        copy_feat(g + (u + 1) // GT, (u + 1) % GT)
                    add(g, u)
                dve.wait_ge(s_st, 16 * (g + 1))
                norm.apply(dve, g, ob).then_inc(s_o, 1)
                dve.wait_ge(s_o, g + 1)
            copy_feat(0, 0)
            groups(dve, group)


def final_phase(nc, h, x, out):
    N, F = x.shape
    NG = N // P // GT
    with ExitStack() as ctx:
        s = Scope(nc, ctx, "fn")
        norm = Norm(s, F)
        hin = [s.sb(f"hin{p}", [P, GT, F], F32) for p in range(2)]
        xin = [s.sb(f"xin{p}", [P, GT, F], F32) for p in range(2)]
        ob = [s.sb(f"ob{p}", [P, GT, F], F32) for p in range(2)]
        s_ld = [s.sem(f"ld{p}") for p in range(2)]
        s_z, s_o = s.sem("z_"), s.sem("o")
        s_st = [s.sem(f"st{p}") for p in range(2)]
        block = ctx.enter_context(nc.Block())

        @block.sync
        def _(sp):
            part = lambda a, g: a.rearrange("(t p) f -> p t f", p=P)[:, bass.ds(GT * g, GT), :]

            def load(g, p):
                sp.dma_start(hin[p][:, :, :], part(h, g)).then_inc(s_ld[p], 16)
                sp.dma_start(xin[p][:, :, :], part(x, g)).then_inc(s_ld[p], 16)

            def store(g, p):
                sp.wait_ge(s_o, g + 1)
                sp.dma_start(part(out, g), ob[p][:, :, :]).then_inc(s_st[p], 16)
            for p in range(2):
                load(p, p)
            with sp.Fori(0, NG // 2 - 1) as g2:
                for p in range(2):
                    sp.wait_ge(s_z, 2 * g2 + p + 1)
                    load(2 * g2 + p + 2, p)
                    store(2 * g2 + p, p)
            for p in range(2):
                store(NG - 2 + p, p)
            for p in range(2):
                sp.wait_ge(s_st[p], 16 * (NG // 2 + 1))

        @block.scalar
        def _(act):
            norm.warm_up(act)
            with act.Fori(0, NG) as g:
                norm.root(act, g)

        @block.vector
        def _(dve):
            norm.fill(dve)
            for p in range(2):
                dve.sem_inc(s_st[p], 16)
            with dve.Fori(0, NG // 2) as g2:
                for p in range(2):
                    g = 2 * g2 + p
                    dve.wait_ge(s_ld[p], 32 * (g2 + 1))
                    dve.tensor_tensor(norm.z[:, :, :], hin[p][:, :, :], xin[p][:, :, :], ALU.add).then_inc(s_z, 1)
                    dve.wait_ge(s_z, g + 1)
                    norm.stats(dve, g, range(GT))
                    dve.wait_ge(s_st[p], 16 * (g2 + 1))
                    norm.apply(dve, g, ob[p]).then_inc(s_o, 1)
                    dve.wait_ge(s_o, g + 1)


def program(nc, x, adj, W0, a1, a2, W_out, b_out, W1, a_pair, out):
    N, F = x.shape
    H0, _, D0 = W0.shape
    H1, _, D1 = W1.shape
    NT = N // P
    dram = lambda name, *shape: nc.dram_tensor(name, shape, F32).ap()
    feat, x1, h1 = dram("feat", N, H0 * D0), dram("x1", N, F), dram("h1", N, H1 * D1)
    with ExitStack() as ctx:
        mask_t = ctx.enter_context(nc.sbuf_tensor("mask_t", [P, NT, N], U8))
        for tag, xs, W, pair, H, D, dst in (("l0", x, W0, (a1, a2), H0, D0, feat),
                                            ("l1", x1, W1, (a_pair[:, 0:D1], a_pair[:, D1:]), H1, D1, h1)):
            d = {"wh": dram(tag + "_wh", N, H * D), "srow": dram(tag + "_srow", H * N),
                 "kcol": dram(tag + "_kcol", H, P, NT),
                 "ncol": dram(tag + "_ncol", H, P, NT)}
            if tag == "l0":
                d["mean"] = dram("mean", 1, H * D)
            with ExitStack() as inner:
                facs = {n: inner.enter_context(nc.sbuf_tensor(f"{tag}_{n}", [P, H, NT], F32))
                        for n in ("eu", "ev", "sb", "sc")}
                prep_phase(nc, tag + "p", xs, W, pair[0], pair[1], d, facs,
                           adj=adj if tag == "l0" else None, mask_t=mask_t)
                attention_phase(nc, tag + "a", mask_t, d, facs, N, H, D, dst, elu=tag == "l0",
                                **PLANS[tag])
            if tag == "l0":
                project_phase(nc, feat, W_out, b_out, x, x1)
    final_phase(nc, h1, x1, out)


_INS = ["x", "adj", "L0_gnn_W_heads", "L0_gnn_a1", "L0_gnn_a2", "L0_gnn_W_out", "L0_gnn_b_out", "L1_gnn_W", "L1_gnn_a"]


def kernel(**inputs):
    import concourse.bacc as bacc
    from concourse.bass_utils import run_bass_kernel_spmd

    nc = bacc.Bacc("TRN2", target_bir_lowering=False, num_devices=1, dynamic_dma_scratch_size=1024)
    arrays, aps = {}, []
    for name in _INS:
        a = np.ascontiguousarray(inputs[name])
        arrays["in_" + name] = a
        aps.append(nc.dram_tensor("in_" + name, a.shape, mybir.dt.from_np(a.dtype), kind="ExternalInput").ap())
    out = nc.dram_tensor("out_0", inputs["x"].shape, F32, kind="ExternalOutput").ap()
    program(nc, *aps, out)
    return run_bass_kernel_spmd(nc, [arrays], core_ids=[0]).results[0]["out_0"]
```
